# Optimizing a Trainium2 kernel written in Bass

```python
import numpy as np
import jax
import jax.numpy as jnp

def _softmax(x, axis=-1):
    return jax.nn.softmax(x, axis=axis)

def _gelu(x):
    return jax.nn.gelu(x, approximate=True)

def _silu(x):
    return jax.nn.silu(x)

def _sigmoid(x):
    return jax.nn.sigmoid(x)

def _layernorm(x, axis=-1, eps=1e-05):
    m = jnp.mean(x, axis=axis, keepdims=True)
    v = jnp.var(x, axis=axis, keepdims=True)
    return (x - m) / jnp.sqrt(v + eps)

def _scatter_add(tgt, idx, src, axis=0):
    return tgt.at[idx].add(src)

def _segment_sum(src, seg, n):
    return jax.ops.segment_sum(src, seg, n)
kernel_name = 'mk_xattn_ffn_d1_seqx_r2_0ffeea'

def setup_inputs(seed: int=0):
    np.random.seed(seed)
    _w = jnp.asarray

    def _rec_inputs():
        import jax
        import jax.numpy as jnp
        _rk = jax.random.key(seed)
        x = -0.0002928 + 1 * jax.random.normal(jax.random.fold_in(_rk, 1), (4, 1024, 512), jnp.float32)
        _lenS = 1024 - jax.random.randint(jax.random.fold_in(_rk, 7), (4,), 0, max(1, 1024 // 4) + 1, jnp.int32)
        _lenS2 = 1024 - jax.random.randint(jax.random.fold_in(_rk, 8), (4,), 0, max(1, 1024 // 4) + 1, jnp.int32)
        _ctx_1024P = jax.random.normal(jax.random.fold_in(_rk, 11), (4, 16, 512), jnp.float32)
        _ctx_1024c = jax.random.dirichlet(jax.random.fold_in(_rk, 511), 0.3 * jnp.ones((16,), jnp.float32), (4, 1024))
        _ctx_1024t = jnp.einsum('bsk,bkd->bsd', _ctx_1024c, _ctx_1024P)
        _ctx_1024t = _ctx_1024t * jax.lax.rsqrt(jnp.mean(jnp.square(_ctx_1024t)) + 1e-12) * 0.953939
        ctx_1024 = -1.39393e-06 + 0.999914 * (_ctx_1024t + 0.3 * jax.random.normal(jax.random.fold_in(_rk, 611), (4, 1024, 512), jnp.float32))
        return (x, ctx_1024)
    x, ctx_1024 = _rec_inputs()

    def _L0_xattn_setup():
        import jax, jax.numpy as jnp
        import numpy as np
        EMBED_PHI = 512
        EMBED_F = 512
        HIDDEN_F = 512
        N_HEADS = 16
        B, S = (2, 1024)
        key = jax.random.key(seed)
        ks = jax.random.split(key, 9)
        sphi = 1.0 / np.sqrt(EMBED_PHI)
        sf = 1.0 / np.sqrt(EMBED_F)
        sh = 1.0 / np.sqrt(HIDDEN_F)
        return {'q': jax.random.normal(ks[0], (B, S, EMBED_PHI), jnp.float32), 'k': jax.random.normal(ks[1], (B, S, EMBED_PHI), jnp.float32), 'v': jax.random.normal(ks[2], (B, S, EMBED_F), jnp.float32), 'Wq': jax.random.normal(ks[3], (HIDDEN_F, EMBED_PHI), jnp.float32) * sphi, 'Wk': jax.random.normal(ks[4], (HIDDEN_F, EMBED_PHI), jnp.float32) * sphi, 'Wv': jax.random.normal(ks[5], (HIDDEN_F, EMBED_F), jnp.float32) * sf, 'bv': jax.random.normal(ks[6], (HIDDEN_F,), jnp.float32) * sf, 'Wo': jax.random.normal(ks[7], (EMBED_F, HIDDEN_F), jnp.float32) * sh, 'bo': jax.random.normal(ks[8], (EMBED_F,), jnp.float32) * sh}
    _L0_xattn_all = _L0_xattn_setup()
    _L0_xattn_in = {k: v for k, v in _L0_xattn_all.items() if k in ('Wq', 'Wk', 'Wv', 'bv', 'Wo', 'bo')}
    del _L0_xattn_all

    def _L0_ffn_setup():
        import jax, jax.numpy as jnp
        import numpy as np
        DM = 512
        NEXPERTS = 32
        EXPERTSETS = 4
        EXPERTSIZE = 32
        BATCH, SEQ = (4, 1024)
        key = jax.random.key(seed)
        k0, k1, k2, k3 = jax.random.split(key, 4)
        scale = 0.02
        x = jax.random.normal(k0, (BATCH, SEQ, DM), jnp.float32)
        controller = jax.random.normal(k1, (DM, NEXPERTS, EXPERTSETS), jnp.float32) * scale
        f1 = jax.random.normal(k2, (DM, NEXPERTS, EXPERTSETS, EXPERTSIZE), jnp.float32) * scale
        bias = jnp.zeros((NEXPERTS, EXPERTSETS, EXPERTSIZE), jnp.float32)
        f2 = jax.random.normal(k3, (NEXPERTS, EXPERTSETS, EXPERTSIZE, DM), jnp.float32) * scale
        return {'x': x, 'controller': controller, 'f1': f1, 'bias': bias, 'f2': f2}
    _L0_ffn_all = _L0_ffn_setup()
    _L0_ffn_in = {k: v for k, v in _L0_ffn_all.items() if k in ('controller', 'f1', 'bias', 'f2')}
    del _L0_ffn_all
    return {'x': x, 'ctx_1024': ctx_1024, 'L0_xattn_Wq': _L0_xattn_in['Wq'], 'L0_xattn_Wk': _L0_xattn_in['Wk'], 'L0_xattn_Wv': _L0_xattn_in['Wv'], 'L0_xattn_bv': _L0_xattn_in['bv'], 'L0_xattn_Wo': _L0_xattn_in['Wo'], 'L0_xattn_bo': _L0_xattn_in['bo'], 'L0_ffn_controller': _L0_ffn_in['controller'], 'L0_ffn_f1': _L0_ffn_in['f1'], 'L0_ffn_bias': _L0_ffn_in['bias'], 'L0_ffn_f2': _L0_ffn_in['f2']}

def reference(x, ctx_1024, L0_xattn_Wq, L0_xattn_Wk, L0_xattn_Wv, L0_xattn_bv, L0_xattn_Wo, L0_xattn_bo, L0_ffn_controller, L0_ffn_f1, L0_ffn_bias, L0_ffn_f2):
    import jax
    import jax.numpy as jnp

    def _L0_xattn_ref(q, k, v, Wq, Wk, Wv, bv, Wo, bo):
        import jax, jax.numpy as jnp
        import numpy as np
        EMBED_PHI = 512
        EMBED_F = 512
        HIDDEN_F = 512
        N_HEADS = 16
        B, S = (2, 1024)
        Bq, Sq, _ = q.shape
        hd = HIDDEN_F // N_HEADS
        scale = 1.0 / np.sqrt(hd)
        qh = (q @ Wq.T).reshape(Bq, Sq, N_HEADS, hd).transpose(0, 2, 1, 3)
        kh = (k @ Wk.T).reshape(Bq, Sq, N_HEADS, hd).transpose(0, 2, 1, 3)
        vh = (v @ Wv.T + bv).reshape(Bq, Sq, N_HEADS, hd).transpose(0, 2, 1, 3)
        scores = jnp.einsum('bhsd,bhtd->bhst', qh, kh) * scale
        mask = jnp.triu(jnp.ones((Sq, Sq), dtype=bool), k=0).at[0, 0].set(False)
        scores = jnp.where(mask, -jnp.inf, scores)
        probs = jax.nn.softmax(scores, axis=-1)
        out = jnp.einsum('bhst,bhtd->bhsd', probs, vh)
        out = out.transpose(0, 2, 1, 3).reshape(Bq, Sq, HIDDEN_F)
        return out @ Wo.T + bo

    def _L0_ffn_ref(x, controller, f1, bias, f2):
        import jax, jax.numpy as jnp
        import numpy as np
        DM = 512
        NEXPERTS = 32
        EXPERTSETS = 4
        EXPERTSIZE = 32
        BATCH, SEQ = (4, 1024)
        B, L, d = x.shape
        t = controller.shape[1]
        g = L // t
        grouped = x.reshape(B, g, t, d)
        logits = jnp.einsum('bgtd,des->bgtes', grouped, controller)
        tie = jnp.linspace(0.0, 1e-06, t, dtype=logits.dtype).reshape(t, 1, 1)
        logits = logits + tie
        perm = (logits == jnp.max(logits, axis=-3, keepdims=True)).astype(x.dtype)
        perm = jax.lax.stop_gradient(perm)
        dispatched = jnp.einsum('bgtd,bgtes->bgesd', grouped, perm)
        inner = jax.nn.relu(jnp.einsum('bgesd,desf->bgesf', dispatched, f1) + bias)
        intermediate = jnp.einsum('bgesf,esfd->bgesd', inner, f2)
        out = jnp.einsum('bgesd,bgtes->bgtd', intermediate, perm)
        return out.reshape(B, L, d)
    x = x + _L0_xattn_ref(_layernorm(x, axis=-1), ctx_1024, ctx_1024, L0_xattn_Wq, L0_xattn_Wk, L0_xattn_Wv, L0_xattn_bv, L0_xattn_Wo, L0_xattn_bo)
    x = x + _L0_ffn_ref(_layernorm(x, axis=-1), L0_ffn_controller, L0_ffn_f1, L0_ffn_bias, L0_ffn_f2)
    return x

_drawn_inputs = setup_inputs


def setup_inputs(seed=0):
    import zlib

    import numpy as np

    out = dict(_drawn_inputs(seed))
    spreads = {'L0_ffn_bias': (0.0, 0.588)}
    factors = {}
    for name, (base, spread) in spreads.items():
        noise = np.random.default_rng([zlib.crc32(name.encode()), seed]).standard_normal(out[name].shape)
        drawn = base * np.exp(spread * noise) if base else spread * noise
        out[name] = jnp.asarray(drawn.astype(out[name].dtype))
    for name, factor in factors.items():
        out[name] = (out[name] * factor).astype(out[name].dtype)
    return out
```

```python
from contextlib import ExitStack

import concourse.bass as bass
from concourse import mybir

F32 = mybir.dt.float32
F32R = mybir.dt.float32r
BF16 = mybir.dt.bfloat16
ALU = mybir.AluOpType
ACT = mybir.ActivationFunctionType
AX = mybir.AxisListType

P = 128
B, S, D = 4, 1024, 512
H, HD = 16, 32
HG = 4
NG = H // HG
T = B * S
CH = 512
NCH = T // CH
KD = D // P
TT = CH // P
E, ES = 32, 4
NE = E * ES
F = 32
GT = E
NGR = T // GT
E4 = NE // 4
EPS = 1e-5
SCALE = float(HD) ** -0.5
MASKED = -1e30


class Plan:
    pass


def scratch(nc):
    m = Plan()
    m.q_hi = nc.dram_tensor("q_hi", (NG, P, T), F32).ap()
    m.q_lo = nc.dram_tensor("q_lo", (NG, P, T), F32).ap()
    m.k_hi = nc.dram_tensor("k_hi", (NG, P, T), F32).ap()
    m.k_lo = nc.dram_tensor("k_lo", (NG, P, T), F32).ap()
    m.v = nc.dram_tensor("v_rows", (T, D), F32).ap()
    m.o = nc.dram_tensor("o_t", (NG, P, T), F32).ap()
    m.pick = nc.dram_tensor("pick_rows", (T // P, NE, P), F32).ap()
    m.x2 = nc.dram_tensor("x_mid", (T, D), F32).ap()
    m.y = nc.dram_tensor("expert_out", (NGR, NE, D), F32).ap()
    return m


def held(eng, value):
    return value if isinstance(value, int) else eng.snap(value)


def project(nc, a, m):
    with ExitStack() as ctx:
        def sb(name, shape, dt):
            return ctx.enter_context(nc.sbuf_tensor(name, shape, dt))

        def sem(name):
            return ctx.enter_context(nc.semaphore(name))

        w_raw = sb("w_raw", [P, 3, KD, D], F32)
        w_hi = sb("w_hi", [P, 3, KD, D], F32R)
        w_lo = sb("w_lo", [P, 3, KD, D], F32R)
        bv_row = sb("bv_row", [P, D], F32)
        ident = sb("ident", [P, P], F32)
        x_in = sb("x_in", [P, TT, D], F32)
        xn = sb("xn", [P, TT, D], F32)
        c_in = sb("c_in", [P, KD, CH], F32)
        c_hi = sb("c_hi", [P, KD, CH], F32R)
        c_lo = sb("c_lo", [P, KD, CH], F32R)
        t_hi = sb("t_hi", [P, KD, CH], F32R)
        t_lo = sb("t_lo", [P, KD, CH], F32R)
        k_hi = sb("k_hi_s", [P, NG, CH], F32R)
        k_lo = sb("k_lo_s", [P, NG, CH], F32R)
        q_hi = sb("q_hi_s", [P, NG, CH], F32R)
        q_lo = sb("q_lo_s", [P, NG, CH], F32R)
        v_out = sb("v_out", [P, TT, D], F32)
        stats = sb("stats", [P, TT, 6], F32)
        mv = sb("mv", [P, TT, 2], F32)
        ve = sb("ve", [P, TT], F32)
        sd = sb("sd", [P, TT], F32)
        r0 = sb("r0", [P, TT], F32)
        r1 = sb("r1", [P, TT], F32)
        r2 = sb("r2", [P, TT], F32)
        rstd = sb("rstd", [P, TT], F32)
        gate = sb("gate", [P, 1], F32)
        bank = ctx.enter_context(nc.psum_tensor("p1_bank", [P, 8, 512], F32))

        w_in = sem("w_in")
        w_split = sem("w_split")
        x_loaded = sem("x_loaded")
        c_loaded = sem("c_loaded")
        c_hi_done = sem("c_hi_done")
        c_lo_done = sem("c_lo_done")
        chain = sem("chain")
        sd_ready = sem("sd_ready")
        xn_ready = sem("xn_ready")
        filled = sem("filled")
        hi_done = sem("hi_done")
        lo_done = sem("lo_done")
        k_stored = sem("k_stored")
        q_stored = sem("q_stored")
        v_stored = sem("v_stored")

        xr = a.x.rearrange("b s d -> (b s) d").rearrange("(c t p) d -> c p t d", t=TT, p=P)
        cr = a.ctx_t.rearrange("c (k p) s -> c p k s", p=P)
        vr = m.v.rearrange("(c t p) d -> c p t d", t=TT, p=P)

        by_chunk = {n: x.rearrange("g p (c s) -> c p g s", c=NCH) for n, x in
                    (("k_hi", m.k_hi), ("k_lo", m.k_lo), ("q_hi", m.q_hi), ("q_lo", m.q_lo))}

        GPC = 16
        APC = 12
        CHAIN = 8

        with nc.Block() as block:
            @block.sync
            def _(sp):
                for i, w in enumerate((a.wq_t, a.wk_t, a.wv_t)):
                    sp.dma_start(w_raw[:, i], w.rearrange("(k p) n -> p k n", p=P)).then_inc(w_in, 16)
                sp.dma_start(ident[:], a.ident).then_inc(w_in, 16)
                sp.dma_start(bv_row[:], a.bv.unsqueeze(0).broadcast_to([P, D])).then_inc(w_in, 16)
                sp.dma_start(x_in[:], xr[0]).then_inc(x_loaded, 16)
                sp.dma_start(c_in[:], cr[0]).then_inc(c_loaded, 16)

                def body(c, last):
                    cur, nxt = held(sp, c), held(sp, c + 1)
                    x_free, k_done = held(sp, c * TT + TT), held(sp, c * GPC + 8)
                    v_done, q_done = held(sp, c * GPC + 12), held(sp, c * GPC + 16)
                    if not last:
                        sp.wait_ge(xn_ready, x_free)
                        sp.dma_start(x_in[:], xr[nxt]).then_inc(x_loaded, 16)
                        sp.wait_ge(c_lo_done, nxt)
                        sp.dma_start(c_in[:], cr[nxt]).then_inc(c_loaded, 16)
                    sp.wait_ge(lo_done, k_done)
                    sp.dma_start(by_chunk["k_hi"][cur], k_hi[:].bitcast(F32)).then_inc(k_stored, 16)
                    sp.dma_start(by_chunk["k_lo"][cur], k_lo[:].bitcast(F32)).then_inc(k_stored, 16)
                    sp.wait_ge(lo_done, v_done)
                    sp.dma_start(vr[cur], v_out[:]).then_inc(v_stored, 16)
                    sp.wait_ge(lo_done, q_done)
                    sp.dma_start(by_chunk["q_hi"][cur], q_hi[:].bitcast(F32)).then_inc(q_stored, 16)
                    sp.dma_start(by_chunk["q_lo"][cur], q_lo[:].bitcast(F32)).then_inc(q_stored, 16)

                with sp.Fori(0, NCH - 1) as c:
                    body(c, False)
                body(NCH - 1, True)
                sp.wait_ge(k_stored, 32 * NCH)
                sp.wait_ge(v_stored, 16 * NCH)
                sp.wait_ge(q_stored, 32 * NCH)

            @block.scalar
            def _(act):
                act.wait_ge(w_in, 80)
                for i in range(3):
                    act.copy(w_hi[:, i], w_raw[:, i]).then_inc(w_split, 1)

                def next_chunk_sd(c):
                    act.wait_ge(chain, c * CHAIN + 3)
                    act.activation(sd[:], ve[:], ACT.Sqrt).then_inc(sd_ready, 1)

                def next_chunk_hi(c, first):
                    act.wait_ge(c_loaded, 16 * c + 16)
                    if not first:
                        act.wait_ge(filled, (c - 1) * GPC + 12)
                    act.copy(c_hi[:], c_in[:]).then_inc(c_hi_done, 1)

                next_chunk_sd(0)
                next_chunk_hi(0, True)

                def body(c, first, last):
                    for k in range(KD):
                        act.wait_ge(filled, c * GPC + k + 1)
                        act.copy(t_hi[:, k], bank[:, k]).then_inc(hi_done, 1)
                    for g in range(NG):
                        act.wait_ge(filled, c * GPC + 4 + g + 1)
                        if not first and g == 0:
                            act.wait_ge(k_stored, 32 * c)
                        act.copy(k_hi[:, g], bank[:, 4 + g]).then_inc(hi_done, 1)
                    if not last:
                        next_chunk_sd(c + 1)
                        next_chunk_hi(c + 1, False)
                    for g in range(NG):
                        act.wait_ge(filled, c * GPC + 12 + g + 1)
                        if not first and g == 0:
                            act.wait_ge(q_stored, 32 * c)
                        act.copy(q_hi[:, g], bank[:, 4 + g]).then_inc(hi_done, 1)

                body(0, True, False)
                with act.Fori(1, NCH - 1) as c:
                    body(c, False, False)
                body(NCH - 1, False, True)

            @block.vector
            def _(dve):
                def link(c, n, ins):
                    ins.then_inc(chain, 1)
                    dve.wait_ge(chain, c * CHAIN + n)

                def ln_rstd(c, n):
                    dve.wait_ge(sd_ready, c + 1)
                    link(c, n, dve.reciprocal(r0[:], sd[:]))
                    link(c, n + 1, dve.tensor_tensor(r1[:], r0[:], r0[:], ALU.mult))
                    link(c, n + 2, dve.tensor_tensor(r2[:], r1[:], ve[:], ALU.mult))
                    link(c, n + 3, dve.tensor_scalar(r1[:], r2[:], -0.5, 1.5, ALU.mult, ALU.add))
                    link(c, n + 4, dve.tensor_tensor(rstd[:], r0[:], r1[:], ALU.mult))

                def ln_apply(c, t, first):
                    if not first and t == 0:
                        dve.wait_ge(filled, (c - 1) * GPC + 4)
                    dve.tensor_scalar(xn[:, t], x_in[:, t], mv[:, t, 0:1], rstd[:, t:t + 1],
                                      ALU.subtract, ALU.mult).then_inc(xn_ready, 1)

                def ctx_lo(c, first):
                    dve.wait_ge(c_hi_done, c + 1)
                    dve.tensor_tensor(c_lo[:], c_in[:], c_hi[:].bitcast(F32), ALU.subtract).then_inc(c_lo_done, 1)

                def stats_all(c):
                    dve.wait_ge(x_loaded, 16 * c + 16)
                    for t in range(TT):
                        ins = dve.bn_stats(stats[:, t], x_in[:, t])
                    link(c, 1, ins)
                    dve.memset(gate[:], 0.0)
                    for t in range(TT):
                        ins = dve.bn_aggr(mv[:, t], stats[:, t])
                    link(c, 2, ins)
                    link(c, 3, dve.tensor_scalar(ve[:], mv[:, :, 1], EPS, None, ALU.add))

                stats_all(0)
                ln_rstd(0, 4)
                for t in range(TT):
                    ln_apply(0, t, True)
                ctx_lo(0, True)
                dve.wait_ge(w_split, 3)
                for i in range(3):
                    dve.tensor_tensor(w_lo[:, i], w_raw[:, i], w_hi[:, i].bitcast(F32), ALU.subtract).then_inc(w_split, 1)

                def body(c, first, last):
                    for k in range(KD):
                        dve.wait_ge(hi_done, c * APC + k + 1)
                        dve.tensor_tensor(t_lo[:, k], bank[:, k], t_hi[:, k].bitcast(F32),
                                          ALU.subtract).then_inc(lo_done, 1)
                    for g in range(NG):
                        dve.wait_ge(hi_done, c * APC + 4 + g + 1)
                        dve.tensor_tensor(k_lo[:, g], bank[:, 4 + g], k_hi[:, g].bitcast(F32),
                                          ALU.subtract).then_inc(lo_done, 1)
                    if not last:
                        stats_all(c + 1)
                    for t in range(TT):
                        dve.wait_ge(filled, c * GPC + 8 + t + 1)
                        if not first and t == 0:
                            dve.wait_ge(v_stored, 16 * c)
                        dve.tensor_tensor(v_out[:, t], bank[:, t], bv_row[:], ALU.add).then_inc(lo_done, 1)
                        if not last and t == 0:
                            ln_rstd(c + 1, 4)
                        if not last:
                            ln_apply(c + 1, t, False)
                    if not last:
                        ctx_lo(c + 1, False)
                    for g in range(NG):
                        dve.wait_ge(hi_done, c * APC + 8 + g + 1)
                        dve.tensor_tensor(q_lo[:, g], bank[:, 4 + g], q_hi[:, g].bitcast(F32),
                                          ALU.subtract).then_inc(lo_done, 1)

                body(0, True, False)
                with dve.Fori(1, NCH - 1) as c:
                    body(c, False, False)
                body(NCH - 1, False, True)

            @block.tensor
            def _(pe):
                pe.wait_ge(w_in, 80)
                pe.wait_ge(w_split, 6)

                def split_product(out, lhs, rhs):
                    for k in range(KD):
                        (lh, ll), (rh, rl) = lhs(k), rhs(k)
                        pe.matmul(out, lh, rh, start=(k == 0), stop=False)
                        pe.matmul(out, lh, rl, start=False, stop=False)
                        mm = pe.matmul(out, ll, rh, start=False, stop=(k == KD - 1))
                    mm.then_inc(filled, 1)

                def body(c, first):
                    pe.wait_ge(xn_ready, c * TT + TT)
                    for k in range(KD):
                        if not first:
                            pe.wait_ge(lo_done, (c - 1) * GPC + 8 + k + 1)
                        for t in range(TT):
                            mm = pe.transpose(bank[:, k, t * P:(t + 1) * P], xn[:, t, k * P:(k + 1) * P], ident[:])
                        mm.then_inc(filled, 1)
                    pe.wait_ge(c_lo_done, c + 1)
                    for g in range(NG):
                        if not first:
                            pe.wait_ge(lo_done, (c - 1) * GPC + 12 + g + 1)
                        split_product(bank[:, 4 + g],
                                      lambda k: [w[:, 1, k, g * P:(g + 1) * P] for w in (w_hi, w_lo)],
                                      lambda k: [c_hi[:, k], c_lo[:, k]])
                    for t in range(TT):
                        pe.wait_ge(lo_done, c * GPC + t + 1)
                        split_product(bank[:, t],
                                      lambda k: [x[:, k, t * P:(t + 1) * P] for x in (c_hi, c_lo)],
                                      lambda k: [w_hi[:, 2, k], w_lo[:, 2, k]])
                    for g in range(NG):
                        pe.wait_ge(lo_done, c * GPC + 4 + g + 1)
                        split_product(bank[:, 4 + g],
                                      lambda k: [w[:, 0, k, g * P:(g + 1) * P] for w in (w_hi, w_lo)],
                                      lambda k: [t_hi[:, k], t_lo[:, k]])

                body(0, True)
                with pe.Fori(1, NCH) as c:
                    body(c, False)


def attend(nc, a, m):
    NIT = B * NG
    ST = S // P
    SLOTS = 3
    R = 3 * HD
    STEPS = [(sh, j) for sh in range(2) for j in range(4 * (sh + 1))]
    NS = len(STEPS)
    CHUNKS = []
    for h in range(HG):
        for i in range(ST):
            if i >= 4:
                CHUNKS.append((h, i, 0, CH, False))
            t0 = CH * (i // 4)
            CHUNKS.append((h, i, t0, (i + 1) * P - t0, True))
    NC = len(CHUNKS)
    MAX_STEPS = 9
    LOADS = 7 * 16
    RP = 4
    AFTER = {8: 0, 11: 1, 14: 2, 17: 3, 30: 4, 33: 5, 36: 6, 39: 7}

    with ExitStack() as ctx:
        def sb(name, shape, dt):
            return ctx.enter_context(nc.sbuf_tensor(name, shape, dt))

        def sem(name):
            return ctx.enter_context(nc.semaphore(name))

        ks = [sb(f"k_stack{i}", [P, HG, S], F32R) for i in range(SLOTS)]
        qs = [sb(f"q_stack{i}", [P, HG, S], F32R) for i in range(SLOTS)]
        vt = [sb(f"v_tile{i}", [P, ST, P], F32) for i in range(SLOTS)]
        pt = sb("p_t", [P, 2, HG, CH], F32)
        mask_f = sb("mask_f", [P, 4, P], F32)
        mask_ts = sb("mask_ts", [P, 2, P], BF16)
        mask_st = sb("mask_st", [P, 2, P], BF16)
        ident = sb("ident2", [P, P], F32)
        ident_b = sb("ident_b", [P, P], BF16)
        ones = sb("ones", [P, HD], F32)
        mx_a = sb("mx_a", [P, HG * ST], F32)
        mx_b = sb("mx_b", [P, HG * ST], F32)
        mx = sb("mx", [P, HG * ST], F32)
        m_row = sb("m_row", [HG * ST, P], F32R)
        o_sb = sb("o_sb", [P, 2, CH], F32)
        d_sb = sb("d_sb", [P, 2, CH], F32)
        r_sb = sb("r_sb", [P, 2, CH], F32)
        o_n = sb("o_n", [P, 2, CH], F32)
        bank = ctx.enter_context(nc.psum_tensor("p2_bank", [P, 8, 512], F32))
        MX, OB, DB = 4, 6, 7

        const_in = sem("const_in")
        const_ready = sem("const_ready")
        loaded = [sem(f"loaded{i}") for i in range(SLOTS)]
        scored = sem("scored")
        exp_done = sem("exp_done")
        step_done = sem("step_done")
        mx_filled = sem("mx_filled")
        mx_read = sem("mx_read")
        mx_ready = sem("mx_ready")
        mx_turned = sem("mx_turned")
        m_row_ready = sem("m_row_ready")
        m_placed = sem("m_placed")
        o_read = sem("o_read")
        inverted = sem("inverted")
        divided = sem("divided")
        o_stored = [sem(f"o_stored{i}") for i in range(2)]

        def load(eng, it, slot):
            b, g = it // NG, it % NG
            for stack, parts in ((ks[slot], (m.k_hi, m.k_lo, m.k_hi)), (qs[slot], (m.q_hi, m.q_hi, m.q_lo))):
                for r, part in enumerate(parts):
                    src = part.rearrange("g (h p) (b s) -> b g p h s", p=HD, b=B)[b, g]
                    eng.dma_start(stack[r * HD:(r + 1) * HD].bitcast(F32), src).then_inc(loaded[slot], 16)
            src = m.v.rearrange("(b t p) (g n) -> b g p t n", b=B, p=P, g=NG)[b, g]
            eng.dma_start(vt[slot][:], src).then_inc(loaded[slot], 16)

        with nc.Block() as block:
            @block.sync
            def _(sp):
                sp.dma_start(mask_f[:, 0:2], a.mask_ts.rearrange("v t s -> t v s")).then_inc(const_in, 16)
                sp.dma_start(mask_f[:, 2:4], a.mask_st.rearrange("v s t -> s v t")).then_inc(const_in, 16)
                sp.dma_start(ident[:], a.ident).then_inc(const_in, 16)
                load(sp, 0, 0)
                load(sp, 1, 1)

                def place_max(it, slot):
                    sp.wait_ge(m_row_ready, it)
                    sp.dma_start(qs[slot][R:R + 1].rearrange("p h s -> p (h s)").bitcast(F32),
                                 m_row[:].bitcast(F32)).then_inc(m_placed, 16)

                def store(it, half, n):
                    sp.wait_ge(divided, n)
                    sp.dma_start(m.o.rearrange("g p (b s) -> b g p s", b=B)[it // NG, it % NG][:, half * CH:(half + 1) * CH],
                                 o_n[:, half]).then_inc(o_stored[half], 16)

                def body(it, slot, first, last, more):
                    cur, prev, nxt = held(sp, it), held(sp, it - 1), held(sp, it + 1)
                    ahead = held(sp, it + 2)
                    steps, two_it = held(sp, it * NS), held(sp, it * 2)
                    this_half, place_at = held(sp, it * 2 + 1), held(sp, it + 2)
                    if more:
                        if not first:
                            sp.wait_ge(step_done, steps)
                        load(sp, ahead, (slot + 2) % SLOTS)
                    if not first:
                        store(prev, 1, two_it)
                    store(cur, 0, this_half)
                    if not last:
                        place_max(place_at, (slot + 1) % SLOTS)

                place_max(1, 0)
                body(0, 0, True, False, True)
                with sp.Fori(0, (NIT - 4) // SLOTS) as g:
                    for u in range(SLOTS):
                        body(g * SLOTS + (1 + u), (1 + u) % SLOTS, False, False, True)
                for it in range(NIT - 3, NIT):
                    body(it, it % SLOTS, False, it == NIT - 1, it + 2 < NIT)
                store(NIT - 1, 1, 2 * NIT)
                for half in range(2):
                    sp.wait_ge(o_stored[half], 16 * NIT)

            @block.gpsimd
            def _(pool):
                pool.wait_ge(const_in, 48)
                pool.tensor_copy(ident_b[:], ident[:]).then_inc(const_ready, 1)
                pool.tensor_copy(mask_ts[:], mask_f[:, 0:2]).then_inc(const_ready, 1)
                pool.tensor_copy(mask_st[:], mask_f[:, 2:4]).then_inc(const_ready, 1)

                def body(it, first):
                    for half in range(2):
                        pool.wait_ge(inverted, (it * 2 + half) * RP + RP)
                        if not first:
                            pool.wait_ge(o_stored[half], it * 16)
                        pool.tensor_tensor(o_n[:, half], o_sb[:, half], r_sb[:, half], ALU.mult).then_inc(divided, 1)

                body(0, True)
                with pool.Fori(1, NIT) as it:
                    body(it, False)

            @block.vector
            def _(dve):
                dve.memset(ones[:], 1.0).then_inc(const_ready, 1)
                dve.memset(mx_b[:], -3e38).then_inc(const_ready, 1)
                for i in range(SLOTS):
                    dve.memset(ks[i][R:R + 1].bitcast(F32), 1.0).then_inc(const_ready, 1)
                dve.wait_ge(const_ready, 8)

                def invert(hf, half, q, first):
                    if q == 0:
                        dve.wait_ge(o_read, hf * 2 + 2)
                        if not first:
                            dve.wait_ge(divided, hf - 1)
                    dve.reciprocal(r_sb[:, half, q * P:(q + 1) * P], d_sb[:, half, q * P:(q + 1) * P]
                                   ).then_inc(inverted, 1)

                def maxima(it, first, older, older_first):
                    for n, (h, i, t0, w, diag) in enumerate(CHUNKS):
                        if n == 0 and not first:
                            dve.wait_ge(mx_ready, it)
                        dve.wait_ge(mx_filled, it * NC + n + 1)
                        to = mx_a if t0 == 0 else mx_b
                        dve.tensor_reduce(to[:, h * ST + i:h * ST + i + 1], bank[:, MX + n % 2, 0:w], AX.X,
                                          ALU.max).then_inc(mx_read, 1)
                        if n in AFTER and not first:
                            q = AFTER[n]
                            if q < RP and older:
                                invert(it * 2 - 3, 1, q, older_first)
                            if q >= RP:
                                invert(it * 2 - 2, 0, q - RP, not older)
                    dve.wait_ge(mx_read, it * NC + NC)
                    if not first:
                        dve.wait_ge(mx_turned, it)
                    dve.tensor_tensor(mx[:], mx_a[:], mx_b[:], ALU.max).then_inc(mx_ready, 1)

                maxima(0, True, False, False)
                maxima(1, False, False, False)
                maxima(2, False, True, True)
                with dve.Fori(3, NIT) as it:
                    maxima(it, False, True, False)
                for hf in range(2 * NIT - 3, 2 * NIT):
                    for q in range(RP):
                        invert(hf, hf % 2, q, False)

            @block.scalar
            def _(act):
                def negate(it, first):
                    act.wait_ge(mx_turned, it + 1)
                    if not first:
                        act.wait_ge(m_placed, it * 16)
                    act.activation(m_row[:], bank[0:HG * ST, MX, 0:P], ACT.Copy, scale=-1.0).then_inc(m_row_ready, 1)

                def take(it, half, first):
                    act.wait_ge(step_done, it * NS + (4 if half == 0 else NS))
                    if not first:
                        act.wait_ge(divided, it * 2 + half - 1)
                    act.copy(o_sb[:, half], bank[:, OB]).then_inc(o_read, 1)
                    act.copy(d_sb[:, half], bank[:, DB]).then_inc(o_read, 1)

                def body(it, first, last):
                    for k, (sh, j) in enumerate(STEPS):
                        w = CH * (sh + 1) - max(CH * sh, P * j)
                        for h in range(HG):
                            act.wait_ge(scored, (it * NS + k) * HG + h + 1)
                            if h == 0 and not (first and k < 2):
                                act.wait_ge(step_done, it * NS + k - 1)
                            act.activation(pt[:, k % 2, h, 0:w], bank[:, h, 0:w], ACT.Exp,
                                           scale=SCALE).then_inc(exp_done, 1)
                        if k == 0 and not first:
                            take(it - 1, 1, False) if not isinstance(it, int) or it > 1 else take(0, 1, True)
                        if k == 4:
                            take(it, 0, first)
                        if k == MAX_STEPS and not last:
                            negate(it + 1, False)

                negate(0, True)
                body(0, True, False)
                body(1, False, False)
                with act.Fori(2, NIT - 1) as it:
                    body(it, False, False)
                body(NIT - 1, False, True)
                take(NIT - 1, 1, False)

            @block.tensor
            def _(pe):
                pe.wait_ge(const_ready, 8)

                def chunk(it, n, slot, first):
                    h, i, t0, w, diag = CHUNKS[n]
                    if n == 0 and not first:
                        pe.wait_ge(m_row_ready, it)
                    if not (first and n < 2):
                        pe.wait_ge(mx_read, it * NC + n - 1)
                    out = bank[:, MX + n % 2, 0:w]
                    mm = pe.matmul(out, qs[slot][0:R, h, i * P:(i + 1) * P], ks[slot][0:R, h, t0:t0 + w],
                                   start=True, stop=not diag)
                    if diag:
                        mm = pe.matmul(bank[:, MX + n % 2, w - P:w], ident_b[:], mask_st[:, 1 if i == 0 else 0],
                                       start=False, stop=True)
                    mm.then_inc(mx_filled, 1)

                def turn(it):
                    pe.wait_ge(mx_ready, it + 1)
                    pe.transpose(bank[0:HG * ST, MX, 0:P], mx[:], ident[:]).then_inc(mx_turned, 1)

                def scores(it, k, slot, first):
                    sh, j = STEPS[k]
                    s0 = max(CH * sh, P * j)
                    w = CH * (sh + 1) - s0
                    diag = P * j >= CH * sh
                    if k == 0:
                        pe.wait_ge(m_placed, it * 16 + 16)
                    for h in range(HG):
                        if not (first and k == 0):
                            pe.wait_ge(exp_done, (it * NS + k - 1) * HG + h + 1)
                        mm = pe.matmul(bank[:, h, 0:w], ks[slot][0:R + 1, h, j * P:(j + 1) * P],
                                       qs[slot][0:R + 1, h, s0:s0 + w], start=True, stop=not diag)
                        if diag:
                            mm = pe.matmul(bank[:, h, 0:P], ident_b[:], mask_ts[:, 1 if j == 0 else 0],
                                           start=False, stop=True)
                        mm.then_inc(scored, 1)

                def values(it, k, slot, first):
                    sh, j = STEPS[k]
                    s0 = max(CH * sh, P * j)
                    w = CH * (sh + 1) - s0
                    c0 = s0 - CH * sh
                    if j == 0 and not (first and sh == 0):
                        pe.wait_ge(o_read, (it * 2 + sh) * 2)
                    for h in range(HG):
                        pe.wait_ge(exp_done, (it * NS + k) * HG + h + 1)
                        pe.matmul(bank[h * HD:(h + 1) * HD, OB, c0:c0 + w], vt[slot][:, j, h * HD:(h + 1) * HD],
                                  pt[:, k % 2, h, 0:w], start=(j == 0), stop=(j == 4 * sh + 3),
                                  tile_position=(0, h * HD), skip_group_check=True)
                    for h in range(HG):
                        mm = pe.matmul(bank[h * HD:(h + 1) * HD, DB, c0:c0 + w], ones[:],
                                       pt[:, k % 2, h, 0:w], start=(j == 0), stop=(j == 4 * sh + 3),
                                       tile_position=(0, h * HD), skip_group_check=True)
                    mm.then_inc(step_done, 1)

                def body(it, slot, first, last, load_count):
                    nslot = (slot + 1) % SLOTS
                    for k in range(NS):
                        if k < NS - 1:
                            scores(it, k + 1, slot, False)
                        elif not last:
                            scores(it + 1, 0, nslot, False)
                        if not last:
                            if k == 0:
                                pe.wait_ge(loaded[nslot], load_count)
                            if k < MAX_STEPS:
                                for n in range(NC * k // MAX_STEPS, NC * (k + 1) // MAX_STEPS):
                                    chunk(it + 1, n, nslot, False)
                            if k == MAX_STEPS:
                                turn(it + 1)
                        values(it, k, slot, first)

                pe.wait_ge(loaded[0], LOADS)
                for n in range(NC):
                    chunk(0, n, 0, True)
                turn(0)
                scores(0, 0, 0, True)
                body(0, 0, True, False, LOADS)
                with pe.Fori(0, (NIT - 4) // SLOTS) as g:
                    for u in range(SLOTS):
                        body(g * SLOTS + (1 + u), (1 + u) % SLOTS, False, False,
                             (g + (2 + u) // SLOTS + 1) * LOADS)
                for it in range(NIT - 3, NIT):
                    body(it, it % SLOTS, False, it == NIT - 1, ((it + 1) // SLOTS + 1) * LOADS)


def dispatch(nc, a, m, inner):
    NT = S // P
    GB = S // GT
    GQ = P // GT
    CHAIN = 7

    with ExitStack() as ctx:
        def sb(name, shape, dt):
            return ctx.enter_context(nc.sbuf_tensor(name, shape, dt))

        def sem(name):
            return ctx.enter_context(nc.semaphore(name))

        f1 = sb("f1_sb", [P, KD, NE * F], F32)
        disp = sb("disp_t", [P, KD, NE, GB], F32)
        wo_raw = disp[:, 0, 0:NE // 2].rearrange("p e g -> p (e g)").rearrange("p (k n) -> p k n", k=KD)
        wo_hi = sb("wo_hi", [P, KD, D], F32R)
        wo_lo = sb("wo_lo", [P, KD, D], F32R)
        ctl = sb("ctl", [P, KD, NE], F32)
        bo_row = sb("bo_row", [P, D], F32)
        bias = sb("bias_sb", [P, E4], F32)
        ident = sb("ident3", [P, P], F32)
        tie = sb("tie", [P, GT], F32)
        blocks = sb("blocks3", [P, GQ], F32)
        o_raw = sb("o_raw", [P, KD, P], F32)
        o_hi = sb("o_hi", [P, 2, KD, P], F32R)
        o_lo = sb("o_lo", [P, 2, KD, P], F32R)
        xb = sb("xb", [P, 2, D], F32)
        x2 = sb("x2", [P, 2, D], F32)
        xn = sb("xn3", [P, D], F32)
        xn_hi = sb("xn_hi", [P, 2, D], F32R)
        xn_lo = sb("xn_lo", [P, 2, D], F32R)
        xn_t = sb("xn_t", [P, 2, KD, P], F32)
        stats = sb("stats3", [P, 6], F32)
        mv = sb("mv3", [P, 2], F32)
        ve = sb("ve3", [P, 1], F32)
        sd = sb("sd3", [P, 1], F32)
        r0 = sb("r03", [P, 1], F32)
        r1 = sb("r13", [P, 1], F32)
        rstd = sb("rstd3", [P, 1], F32)
        gate = sb("gate3", [P, 1], F32)
        logits = sb("logits", [P, P], F32)
        best = sb("best", [P, GQ], F32)
        pick_t = sb("pick_t", [P, 2, P], F32)
        pick = sb("pick", [P, 2, GQ, NE], F32R)
        hid = sb("hid", [P, E4 // 2, GB], F32)
        bank = ctx.enter_context(nc.psum_tensor("p3_bank", [P, 8, 512], F32))
        A, TB, LB, DB, EB, FB = 0, 2, 3, 4, 5, (7, 4)

        const_in = sem("c3_in")
        f1_in = sem("f1_in")
        wo_split = sem("wo_split")
        o_loaded = sem("o_loaded")
        x_loaded = [sem(f"x3_loaded{i}") for i in range(2)]
        x2_stored = [sem(f"x2_stored{i}") for i in range(2)]
        pick_stored = [sem(f"pick_stored{i}") for i in range(2)]
        o_hi_done = sem("o_hi_done")
        o_lo_done = sem("o_lo_done")
        xb_done = sem("xb_done")
        attended = sem("attended")
        x2_done = sem("x2_done")
        chain = sem("chain3")
        sd_done = sem("sd3_done")
        xn_done = sem("xn3_done")
        xn_hi_done = sem("xn3_hi_done")
        xn_lo_done = sem("xn3_lo_done")
        turned = sem("turned")
        xn_t_done = sem("xn_t_done")
        routed = sem("routed")
        tie_done = sem("tie_done")
        best_done = sem("best_done")
        pick_t_done = sem("pick_t_done")
        pick_turned = sem("pick_turned")
        pick_done = sem("pick_done")
        gathered = sem("gathered")
        taken_a = sem("taken_a")
        taken_v = sem("taken_v")
        hidden = sem("hidden")
        biased = sem("biased")
        relued = sem("relued")

        o_src = m.o.rearrange("g p (i s) -> i p g s", s=P)
        x_src = a.x.rearrange("b s d -> (b s) d").rearrange("(i p) d -> i p d", p=P)
        x2_dst = m.x2.rearrange("(i p) d -> i p d", p=P)

        with nc.Block() as block:
            @block.sync
            def _(sp):
                for dst, src in ((wo_raw, a.wo_t.rearrange("(k p) n -> p k n", p=P)),
                                 (ident[:], a.ident), (ctl[:], a.controller.rearrange("(k p) n -> p k n", p=P)),
                                 (bo_row[:], a.bo.unsqueeze(0).broadcast_to([P, D])),
                                 (tie[:], a.tie_row.unsqueeze(0).broadcast_to([P, GT])),
                                 (blocks[:], a.block_cols), (bias[:], a.bias_col)):
                    sp.dma_start(dst, src).then_inc(const_in, 16)

                def load(i, n, first):
                    tile, x_free = held(sp, i), held(sp, i - 1)
                    if not (first and n == 0):
                        sp.wait_ge(o_lo_done, tile)
                    sp.dma_start(o_raw[:], o_src[tile]).then_inc(o_loaded, 16)
                    if not (first and n < 2):
                        sp.wait_ge(x2_done, x_free)
                    sp.dma_start(xb[:, n % 2], x_src[tile]).then_inc(x_loaded[n % 2], 16)

                def store(i, n, first):
                    tile, done = held(sp, i), held(sp, i + 1)
                    sp.wait_ge(x2_done, done)
                    sp.dma_start(x2_dst[tile], x2[:, n % 2]).then_inc(x2_stored[n % 2], 16)

                def store_pick(i, n, first):
                    tile, done = held(sp, i), held(sp, i + 1)
                    sp.wait_ge(pick_t_done, done)
                    sp.dma_start(m.pick[tile], pick_t[:, n % 2]).then_inc(pick_stored[n % 2], 16)

                def body(b, first, last):
                    for n in range(NT):
                        if not (last and n == NT - 1):
                            load(b * NT + n + 1, n + 1, first)
                        store(b * NT + n, n, first)
                        if n > 0:
                            store_pick(b * NT + n - 1, n - 1, first)
                    store_pick(b * NT + NT - 1, NT - 1, first)

                load_f1 = a.f1.rearrange("(k p) n -> p k n", p=P)
                load(0, 0, True)
                sp.dma_start(f1[:], load_f1).then_inc(f1_in, 16)

                body(0, True, False)
                with sp.Fori(1, B - 1) as b:
                    body(b, False, False)
                body(B - 1, False, True)
                for i in range(2):
                    sp.wait_ge(x2_stored[i], 16 * B * NT // 2)
                    sp.wait_ge(pick_stored[i], 16 * B * NT // 2)

            @block.gpsimd
            def _(pool):
                pool.wait_ge(const_in, 16 * 7)

                def body(b, first):
                    for n in range(NT + 1):
                        i = b * NT + n
                        if n < NT:
                            pool.wait_ge(x_loaded[n % 2], (b * (NT // 2) + n // 2) * 16 + 16)
                            pool.tensor_tensor(xb[:, n % 2], xb[:, n % 2], bo_row[:], ALU.add).then_inc(xb_done, 1)
                        if n > 0:
                            pool.wait_ge(xn_hi_done, i)
                            if not (first and n < 3):
                                pool.wait_ge(gathered, (i - 2) * KD)
                            pool.tensor_tensor(xn_lo[:, (n - 1) % 2], xn[:], xn_hi[:, (n - 1) % 2].bitcast(F32),
                                               ALU.subtract).then_inc(xn_lo_done, 1)

                body(0, True)
                with pool.Fori(1, B) as b:
                    body(b, False)

            @block.scalar
            def _(act):
                act.wait_ge(const_in, 16 * 7)
                act.copy(wo_hi[:], wo_raw).then_inc(wo_split, 1)

                def o_part(i, n, first):
                    act.wait_ge(o_loaded, i * 16 + 16)
                    if not (first and n < 2):
                        act.wait_ge(attended, i - 1)
                    act.copy(o_hi[:, n % 2], o_raw[:]).then_inc(o_hi_done, 1)

                def body(b, first, last):
                    for n in range(NT + 2):
                        i = b * NT + n
                        if n < NT - 1 or (n == NT - 1 and not last):
                            o_part(i + 1, n + 1, first)
                        if 1 <= n <= NT:
                            act.wait_ge(turned, i)
                            if not (first and n < 3):
                                act.wait_ge(routed, i - 2)
                            act.copy(xn_t[:, (n - 1) % 2], bank[:, TB]).then_inc(xn_t_done, 1)
                        if n >= 2:
                            for k in (0, 2):
                                act.wait_ge(gathered, (i - 2) * KD + k + 1)
                                if n == 2 and k == 0 and not first:
                                    act.wait_ge(hidden, b * 2)
                                act.copy(disp[:, k, :, (n - 2) * GQ:(n - 1) * GQ].rearrange("p e g -> p g e"),
                                         bank[:, EB].rearrange("p (g e) -> p g e", g=GQ)).then_inc(taken_a, 1)
                        if n < NT:
                            act.wait_ge(chain, i * CHAIN + 3)
                            act.activation(sd[:], ve[:], ACT.Sqrt).then_inc(sd_done, 1)
                            act.wait_ge(xn_done, i + 1)
                            if not (first and n < 2):
                                act.wait_ge(gathered, (i - 1) * KD)
                            act.copy(xn_hi[:, n % 2], xn[:]).then_inc(xn_hi_done, 1)

                o_part(0, 0, True)
                body(0, True, False)
                with act.Fori(1, B - 1) as b:
                    body(b, False, False)
                body(B - 1, False, True)

            @block.vector
            def _(dve):
                dve.wait_ge(const_in, 16 * 7)
                dve.wait_ge(wo_split, 1)
                dve.tensor_tensor(wo_lo[:], wo_raw, wo_hi[:].bitcast(F32), ALU.subtract).then_inc(wo_split, 1)

                def o_part(i, n, first):
                    dve.wait_ge(o_hi_done, i + 1)
                    dve.tensor_tensor(o_lo[:, n % 2], o_raw[:], o_hi[:, n % 2].bitcast(F32),
                                      ALU.subtract).then_inc(o_lo_done, 1)

                def link(i, n, ins):
                    ins.then_inc(chain, 1)
                    dve.wait_ge(chain, i * CHAIN + n)

                def body(b, first, last):
                    for n in range(NT + 2):
                        i = b * NT + n
                        if n < NT - 1 or (n == NT - 1 and not last):
                            o_part(i + 1, n + 1, first)
                        if n >= 2:
                            dve.wait_ge(pick_turned, i - 1)
                            if not (first and n < 4):
                                dve.wait_ge(gathered, (i - 3) * KD)
                            dve.tensor_tensor(pick[:, n % 2],
                                              bank[:, DB, 0:NE].unsqueeze(1).broadcast_to([P, GQ, NE]),
                                              blocks[:].unsqueeze(2).broadcast_to([P, GQ, NE]),
                                              ALU.mult).then_inc(pick_done, 1)
                        if n < NT:
                            dve.wait_ge(attended, i + 1)
                            dve.wait_ge(xb_done, i + 1)
                            if not (first and n < 2):
                                dve.wait_ge(x2_stored[n % 2], (b * (NT // 2) + n // 2) * 16)
                            dve.tensor_tensor(x2[:, n % 2], bank[:, A + n % 2], xb[:, n % 2],
                                              ALU.add).then_inc(x2_done, 1)
                            dve.wait_ge(x2_done, i + 1)
                            link(i, 1, dve.bn_stats(stats[:], x2[:, n % 2]))
                            dve.memset(gate[:], 0.0)
                            link(i, 2, dve.bn_aggr(mv[:], stats[:]))
                            link(i, 3, dve.tensor_scalar(ve[:], mv[:, 1:2], EPS, None, ALU.add))
                        if n >= 2:
                            for k in (1, 3):
                                dve.wait_ge(gathered, (i - 2) * KD + k + 1)
                                dve.tensor_copy(disp[:, k, :, (n - 2) * GQ:(n - 1) * GQ].rearrange("p e g -> p g e"),
                                                bank[:, EB + 1].rearrange("p (g e) -> p g e", g=GQ)
                                                ).then_inc(taken_v, 1)
                        if n < NT:
                            dve.wait_ge(sd_done, i + 1)
                            link(i, 4, dve.reciprocal(r0[:], sd[:]))
                            link(i, 5, dve.scalar_tensor_tensor(r1[:], r0[:], r0[:, 0:1], ve[:], ALU.mult, ALU.mult))
                            link(i, 6, dve.tensor_scalar(r1[:], r1[:], -0.5, 1.5, ALU.mult, ALU.add))
                            link(i, 7, dve.tensor_tensor(rstd[:], r0[:], r1[:], ALU.mult))
                            if not (first and n < 1):
                                dve.wait_ge(xn_lo_done, i)
                                dve.wait_ge(turned, i)
                            dve.tensor_scalar(xn[:], x2[:, n % 2], mv[:, 0:1], rstd[:], ALU.subtract,
                                              ALU.mult).then_inc(xn_done, 1)
                        if 1 <= n <= NT:
                            dve.wait_ge(routed, i)
                            dve.tensor_tensor(logits[:].rearrange("p (g t) -> p g t", g=GQ),
                                              bank[:, LB, 0:P].rearrange("p (g t) -> p g t", g=GQ),
                                              tie[:].unsqueeze(1).broadcast_to([P, GQ, GT]),
                                              ALU.add).then_inc(tie_done, 1)
                            dve.wait_ge(tie_done, i)
                            dve.tensor_reduce(best[:], logits[:].rearrange("p (g t) -> p g t", g=GQ), AX.X,
                                              ALU.max).then_inc(best_done, 1)
                            dve.wait_ge(best_done, i)
                            if not (first and n < 3):
                                dve.wait_ge(pick_stored[(n - 1) % 2], (b * (NT // 2) + (n - 1) // 2) * 16)
                                dve.wait_ge(pick_turned, i - 2)
                            dve.tensor_tensor(pick_t[:, (n - 1) % 2].rearrange("p (g t) -> p g t", g=GQ),
                                              logits[:].rearrange("p (g t) -> p g t", g=GQ),
                                              best[:].unsqueeze(2).broadcast_to([P, GQ, GT]),
                                              ALU.is_equal).then_inc(pick_t_done, 1)
                            dve.wait_ge(pick_t_done, i)
                    for half in range(2):
                        es = slice(half * (E4 // 2), (half + 1) * (E4 // 2))
                        dve.wait_ge(hidden, b * 2 + half + 1)
                        if not (first and half == 0):
                            dve.wait_ge(relued, b * 2 + half)
                        dve.tensor_tensor(hid[:], bank[:, FB[half]].rearrange("p (e g) -> p e g", g=GB),
                                          bias[:, es].unsqueeze(2).broadcast_to([P, E4 // 2, GB]),
                                          ALU.add).then_inc(biased, 1)
                        dve.wait_ge(biased, b * 2 + half + 1)
                        dve.tensor_scalar(inner[:, es, :].rearrange("p e (b g) -> p b e g", b=B)[:, b], hid[:], 0.0,
                                          None, ALU.max).then_inc(relued, 1)

                o_part(0, 0, True)
                body(0, True, False)
                with dve.Fori(1, B - 1) as b:
                    body(b, False, False)
                body(B - 1, False, True)

            @block.tensor
            def _(pe):
                pe.wait_ge(wo_split, 2)

                def body(b, first, last):
                    for n in range(NT + 2):
                        i = b * NT + n
                        if n < NT:
                            pe.wait_ge(o_lo_done, i + 1)
                            if not (first and n < 2):
                                pe.wait_ge(x2_done, i - 1)
                            for k in range(KD):
                                oh, ol = o_hi[:, n % 2, k], o_lo[:, n % 2, k]
                                pe.matmul(bank[:, A + n % 2], oh, wo_hi[:, k], start=(k == 0), stop=False)
                                pe.matmul(bank[:, A + n % 2], oh, wo_lo[:, k], start=False, stop=False)
                                mm = pe.matmul(bank[:, A + n % 2], ol, wo_hi[:, k], start=False, stop=(k == KD - 1))
                            mm.then_inc(attended, 1)
                        if n >= 2:
                            pe.wait_ge(pick_t_done, i - 1)
                            if n == 2 and not first:
                                pe.wait_ge(biased, b * 2)
                            if not (first and n == 2):
                                pe.wait_ge(pick_done, i - 2)
                            pe.transpose(bank[:, DB, 0:P], pick_t[:, n % 2], ident[:]).then_inc(pick_turned, 1)
                        if 1 <= n <= NT:
                            pe.wait_ge(xn_done, i)
                            if not (first and n == 1):
                                pe.wait_ge(xn_t_done, i - 1)
                            for k in range(KD):
                                mm = pe.transpose(bank[:, TB, k * P:(k + 1) * P], xn[:, k * P:(k + 1) * P], ident[:])
                            mm.then_inc(turned, 1)
                        if n >= 2:
                            pe.wait_ge(xn_lo_done, i - 1)
                            pe.wait_ge(pick_done, i - 1)
                            for k in range(KD):
                                if k % 2 == 0:
                                    if not (first and n == 2 and k == 0):
                                        pe.wait_ge(taken_a, (i - 2) * 2 + k // 2)
                                else:
                                    if not (first and n == 2 and k == 1):
                                        pe.wait_ge(taken_v, (i - 2) * 2 + k // 2)
                                out = bank[:, EB + k % 2]
                                rhs = pick[:, n % 2].rearrange("p g e -> p (g e)")
                                pe.matmul(out, xn_hi[:, n % 2, k * P:(k + 1) * P], rhs, start=True, stop=False)
                                pe.matmul(out, xn_lo[:, n % 2, k * P:(k + 1) * P], rhs, start=False,
                                          stop=True).then_inc(gathered, 1)
                        if 1 <= n <= NT:
                            pe.wait_ge(xn_t_done, i)
                            if not (first and n == 1):
                                pe.wait_ge(tie_done, i - 1)
                            for k in range(KD):
                                mm = pe.matmul(bank[:, LB, 0:P], ctl[:, k], xn_t[:, (n - 1) % 2, k],
                                               start=(k == 0), stop=(k == KD - 1))
                            mm.then_inc(routed, 1)
                    if first:
                        pe.wait_ge(f1_in, 16)
                    pe.wait_ge(taken_a, (b * NT + NT) * 2)
                    pe.wait_ge(taken_v, (b * NT + NT) * 2)
                    for half in range(2):
                        if half == 0 and not first:
                            pe.wait_ge(biased, b * 2)
                        if half == 1:
                            pe.wait_ge(pick_done, b * NT + NT)
                        for e in range(E4 // 2):
                            for k in range(KD):
                                for q in range(4):
                                    es = (half * (E4 // 2) + e) * 4 + q
                                    mm = pe.matmul(bank[q * F:(q + 1) * F, FB[half], e * GB:(e + 1) * GB],
                                                   f1[:, k, es * F:(es + 1) * F], disp[:, k, es],
                                                   start=(k == 0), stop=(k == KD - 1), tile_position=(0, q * F),
                                                   skip_group_check=True)
                        mm.then_inc(hidden, 1)

                body(0, True, False)
                with pe.Fori(1, B - 1) as b:
                    body(b, False, False)
                body(B - 1, False, True)


def expand(nc, a, m, inner):
    with ExitStack() as ctx:
        def sb(name, shape, dt):
            return ctx.enter_context(nc.sbuf_tensor(name, shape, dt))

        def sem(name):
            return ctx.enter_context(nc.semaphore(name))

        in_hi = sb("in_hi", [P, E4, NGR], F32R)
        in_lo = sb("in_lo", [P, E4, NGR], F32R)
        blocks = sb("blocks4", [P, 4], F32)
        raw = sb("f2_raw", [P, 2, D], F32)
        w_hi = sb("f2_hi", [P, 2, D], F32R)
        w_lo = sb("f2_lo", [P, 2, D], F32R)
        d_hi = sb("d_hi", [P, 2, 4, NGR], F32R)
        d_lo = sb("d_lo", [P, 2, 4, NGR], F32R)
        y = sb("y_sb", [P, 2, 4, D], F32)
        bank = ctx.enter_context(nc.psum_tensor("p4_bank", [P, 8, 512], F32))

        c_in = sem("c4_in")
        in_split = sem("in_split")
        loaded = [sem(f"f2_loaded{i}") for i in range(2)]
        w_hi_done = sem("f2_hi_done")
        w_lo_done = sem("f2_lo_done")
        d_hi_done = sem("d_hi_done")
        d_lo_done = sem("d_lo_done")
        made = sem("y_made")
        taken_a = sem("y_taken_a")
        taken_v = sem("y_taken_v")
        stored = [sem(f"y_stored{i}") for i in range(2)]

        src = a.f2.rearrange("(e p) d -> e p d", p=P)
        dst = m.y.rearrange("g (e q) d -> e g q d", q=4)

        with nc.Block() as block:
            @block.sync
            def _(sp):
                sp.dma_start(blocks[:], a.block_cols).then_inc(c_in, 16)
                for u in range(2):
                    sp.dma_start(raw[:, u], src[u]).then_inc(loaded[u], 16)

                def body(j, more):
                    for u in range(2):
                        e, ahead = held(sp, j * 2 + u), held(sp, j * 2 + u + 2)
                        split, done = held(sp, j * 2 + u + 1), held(sp, (j * 2 + u + 1) * 2)
                        if more:
                            sp.wait_ge(w_lo_done, split)
                            sp.dma_start(raw[:, u], src[ahead]).then_inc(loaded[u], 16)
                        sp.wait_ge(taken_a, done)
                        sp.wait_ge(taken_v, done)
                        sp.dma_start(dst[e], y[:, u]).then_inc(stored[u], 16)

                with sp.Fori(0, E4 // 2 - 1) as j:
                    body(j, True)
                body(E4 // 2 - 1, False)
                for u in range(2):
                    sp.wait_ge(stored[u], 16 * E4 // 2)

            @block.gpsimd
            def _(pool):
                pool.wait_ge(in_split, 2)

                def body(j, first):
                    for u in range(2):
                        if not first:
                            pool.wait_ge(made, (j * 2 + u - 1) * 4)
                        pool.tensor_tensor(d_lo[:, u],
                                           in_lo[:, j * 2 + u].bitcast(F32).unsqueeze(1).broadcast_to([P, 4, NGR]),
                                           blocks[:].unsqueeze(2).broadcast_to([P, 4, NGR]),
                                           ALU.mult).then_inc(d_lo_done, 1)

                body(0, True)
                with pool.Fori(1, E4 // 2) as j:
                    body(j, False)

            @block.scalar
            def _(act):
                act.copy(in_hi[:], inner[:]).then_inc(in_split, 1)

                def split(e, u, more, first):
                    act.wait_ge(loaded[u], more)
                    if not first:
                        act.wait_ge(made, (e - 1) * 4)
                    act.copy(w_hi[:, u], raw[:, u]).then_inc(w_hi_done, 1)

                def body(j, first, last):
                    for u in range(2):
                        e = j * 2 + u
                        if not (last and u == 1):
                            split(e + 1, (u + 1) % 2, (j + (u + 1) // 2) * 16 + 16, first and u == 0)
                        for q in (0, 1):
                            act.wait_ge(made, e * 4 + q + 1)
                            if not first and q == 0:
                                act.wait_ge(stored[u], j * 16)
                            act.copy(y[:, u, q], bank[:, u * 4 + q]).then_inc(taken_a, 1)

                split(0, 0, 16, True)
                body(0, True, False)
                with act.Fori(1, E4 // 2 - 1) as j:
                    body(j, False, False)
                body(E4 // 2 - 1, False, True)

            @block.vector
            def _(dve):
                dve.wait_ge(c_in, 16)
                dve.wait_ge(in_split, 1)
                dve.tensor_tensor(in_lo[:], inner[:], in_hi[:].bitcast(F32), ALU.subtract).then_inc(in_split, 1)

                def prepare(e, u, first):
                    dve.wait_ge(w_hi_done, e + 1)
                    dve.tensor_tensor(w_lo[:, u], raw[:, u], w_hi[:, u].bitcast(F32), ALU.subtract
                                      ).then_inc(w_lo_done, 1)
                    if not first:
                        dve.wait_ge(made, (e - 1) * 4)
                    dve.tensor_tensor(d_hi[:, u], in_hi[:, e].bitcast(F32).unsqueeze(1).broadcast_to([P, 4, NGR]),
                                      blocks[:].unsqueeze(2).broadcast_to([P, 4, NGR]),
                                      ALU.mult).then_inc(d_hi_done, 1)

                def body(j, first, last):
                    for u in range(2):
                        e = j * 2 + u
                        if not (last and u == 1):
                            prepare(e + 1, (u + 1) % 2, first and u == 0)
                        for q in (2, 3):
                            dve.wait_ge(made, e * 4 + q + 1)
                            if not first and q == 2:
                                dve.wait_ge(stored[u], j * 16)
                            dve.tensor_copy(y[:, u, q], bank[:, u * 4 + q]).then_inc(taken_v, 1)

                prepare(0, 0, True)
                body(0, True, False)
                with dve.Fori(1, E4 // 2 - 1) as j:
                    body(j, False, False)
                body(E4 // 2 - 1, False, True)

            @block.tensor
            def _(pe):
                def body(j, first):
                    for u in range(2):
                        e = j * 2 + u
                        pe.wait_ge(w_lo_done, e + 1)
                        pe.wait_ge(d_hi_done, e + 1)
                        pe.wait_ge(d_lo_done, e + 1)
                        for q in range(4):
                            if not first:
                                if q < 2:
                                    pe.wait_ge(taken_a, (e - 2) * 2 + q + 1)
                                else:
                                    pe.wait_ge(taken_v, (e - 2) * 2 + q - 1)
                            out = bank[:, u * 4 + q]
                            pe.matmul(out, d_hi[:, u, q], w_hi[:, u], start=True, stop=False)
                            pe.matmul(out, d_hi[:, u, q], w_lo[:, u], start=False, stop=False)
                            pe.matmul(out, d_lo[:, u, q], w_hi[:, u], start=False, stop=True).then_inc(made, 1)

                body(0, True)
                with pe.Fori(1, E4 // 2) as j:
                    body(j, False)


def combine(nc, a, m, inner):
    NTL = T // P
    GQ = P // GT
    with ExitStack() as ctx:
        def sb(name, shape, dt):
            return ctx.enter_context(nc.sbuf_tensor(name, shape, dt))

        def sem(name):
            return ctx.enter_context(nc.semaphore(name))

        U = 4
        y = sb("y_in", [P, U, GQ, D], F32)
        pick = sb("pick_in", [P, U, P], F32)
        x2 = sb("x2_in", [P, U, D], F32)
        out = sb("out_sb", [P, U, D], F32)
        bank = ctx.enter_context(nc.psum_tensor("p5_bank", [P, 8, 512], F32))
        loaded = [sem(f"y_loaded{i}") for i in range(U)]
        stored = [sem(f"out_stored{i}") for i in range(U)]
        summed = sem("summed")
        added = sem("added")

        x2_src = m.x2.rearrange("(i p) d -> i p d", p=P)
        y_src = m.y.rearrange("(i g) e d -> i e g d", g=GQ)
        o_dst = a.out.rearrange("b (n p) d -> (b n) p d", p=P)

        with nc.Block() as block:
            @block.sync
            def _(sp):
                def load(i, u):
                    sp.dma_start(y[:, u], y_src[i]).then_inc(loaded[u], 16)
                    sp.dma_start(pick[:, u], m.pick[i]).then_inc(loaded[u], 16)
                    sp.dma_start(x2[:, u], x2_src[i]).then_inc(loaded[u], 16)

                for u in range(U):
                    load(u, u)
                with sp.Fori(0, NTL // U - 1) as j:
                    for u in range(U):
                        ahead, done = held(sp, j * U + U + u), held(sp, j * U + u + 1)
                        sp.wait_ge(added, done)
                        load(ahead, u)

            @block.scalar
            def _(act):
                def body(j):
                    for u in range(U):
                        act.wait_ge(added, j * U + u + 1)
                        act.dma_start(o_dst[j * U + u], out[:, u]).then_inc(stored[u], 16)

                with act.Fori(0, NTL // U) as j:
                    body(j)
                for u in range(U):
                    act.wait_ge(stored[u], 16 * NTL // U)

            @block.vector
            def _(dve):
                def body(j, first):
                    for u in range(U):
                        dve.wait_ge(summed, j * U + u + 1)
                        if not first:
                            dve.wait_ge(stored[u], j * 16)
                        dve.tensor_tensor(out[:, u], bank[:, u], x2[:, u], ALU.add).then_inc(added, 1)

                body(0, True)
                with dve.Fori(1, NTL // U) as j:
                    body(j, False)

            @block.tensor
            def _(pe):
                def body(j, first):
                    for u in range(U):
                        pe.wait_ge(loaded[u], j * 48 + 48)
                        if not first:
                            pe.wait_ge(added, j * U + u - (U - 1))
                        for g in range(GQ):
                            mm = pe.matmul(bank[g * GT:(g + 1) * GT, u], pick[:, u, g * GT:(g + 1) * GT], y[:, u, g],
                                           start=True, stop=True, tile_position=(0, g * GT))
                        mm.then_inc(summed, 1)

                body(0, True)
                with pe.Fori(1, NTL // U) as j:
                    body(j, False)


def build(nc, a, m, phases=(1, 2, 3, 4, 5)):
    if 1 in phases:
        project(nc, a, m)
    if 2 in phases:
        attend(nc, a, m)
    with nc.sbuf_tensor("inner", [P, E4, NGR], F32) as inner:
        for n, phase in ((3, dispatch), (4, expand), (5, combine)):
            if n in phases:
                phase(nc, a, m, inner)


def layout(**inputs):
    import numpy as np

    def arr(x):
        return np.ascontiguousarray(np.asarray(x))

    i = inputs
    ctx = arr(i["ctx_1024"])
    r = np.arange(P)
    ban = np.where(r[:, None] >= r[None, :], np.float32(MASKED), np.float32(0))
    ban0 = ban.copy()
    ban0[0, 0] = 0.0
    out = {
        "x": arr(i["x"]),
        "ctx_t": arr(ctx.reshape(NCH, CH, D).transpose(0, 2, 1)),
        "wq_t": arr(arr(i["L0_xattn_Wq"]).T),
        "wk_t": arr(arr(i["L0_xattn_Wk"]).T),
        "wv_t": arr(arr(i["L0_xattn_Wv"]).T),
        "wo_t": arr(arr(i["L0_xattn_Wo"]).T),
        "bv": arr(i["L0_xattn_bv"]),
        "bo": arr(i["L0_xattn_bo"]),
        "controller": arr(i["L0_ffn_controller"]).reshape(D, NE),
        "f1": arr(i["L0_ffn_f1"]).reshape(D, NE * F),
        "bias_col": arr(arr(i["L0_ffn_bias"]).reshape(E4, P).T),
        "f2": arr(i["L0_ffn_f2"]).reshape(NE * F, D),
        "ident": np.eye(P, dtype=np.float32),
        "mask_ts": np.stack([ban, ban0]),
        "mask_st": arr(np.stack([ban.T, ban0.T])),
        "tie_row": np.linspace(0.0, 1e-6, GT, dtype=np.float32),
        "block_cols": arr((r[:, None] // 32 == np.arange(4)[None, :]).astype(np.float32)),
    }
    return out


def kernel(**inputs):
    import numpy as np
    import concourse.bacc as bacc
    from concourse.bass_utils import run_bass_kernel_spmd

    nc = bacc.Bacc("TRN2", target_bir_lowering=False, num_devices=1)
    arrays, a = {}, Plan()
    for name, x in layout(**inputs).items():
        arrays["in_" + name] = x
        a.__dict__[name] = nc.dram_tensor("in_" + name, x.shape, mybir.dt.from_np(x.dtype), kind="ExternalInput").ap()
    a.out = nc.dram_tensor("out", (B, S, D), F32, kind="ExternalOutput").ap()
    build(nc, a, scratch(nc))
    r = run_bass_kernel_spmd(nc, [arrays], core_ids=[0])
    return r.results[0]["out"]
```

```python
from contextlib import ExitStack

import concourse.bass as bass
from concourse import mybir

F32 = mybir.dt.float32
F32R = mybir.dt.float32r
BF16 = mybir.dt.bfloat16
ALU = mybir.AluOpType
ACT = mybir.ActivationFunctionType
AX = mybir.AxisListType

P = 128
B, S, D = 4, 1024, 512
H, HD = 16, 32
HG = 4
NG = H // HG
T = B * S
CH = 512
NCH = T // CH
KD = D // P
TT = CH // P
E, ES = 32, 4
NE = E * ES
F = 32
GT = E
NGR = T // GT
E4 = NE // 4
EPS = 1e-5
SCALE = float(HD) ** -0.5
MASKED = -1e30


class Plan:
    pass


def scratch(nc):
    m = Plan()
    m.q_hi = nc.dram_tensor("q_hi", (NG, P, T), F32).ap()
    m.q_lo = nc.dram_tensor("q_lo", (NG, P, T), F32).ap()
    m.k_hi = nc.dram_tensor("k_hi", (NG, P, T), F32).ap()
    m.k_lo = nc.dram_tensor("k_lo", (NG, P, T), F32).ap()
    m.v = nc.dram_tensor("v_rows", (T, D), F32).ap()
    m.o = nc.dram_tensor("o_t", (NG, P, T), F32).ap()
    m.pick = nc.dram_tensor("pick_rows", (T // P, NE, P), F32).ap()
    m.x2 = nc.dram_tensor("x_mid", (T, D), F32).ap()
    m.y = nc.dram_tensor("expert_out", (NGR, NE, D), F32).ap()
    return m


def held(eng, value):
    return value if isinstance(value, int) else eng.snap(value)


def project(nc, a, m):
    with ExitStack() as ctx:
        def sb(name, shape, dt):
            return ctx.enter_context(nc.sbuf_tensor(name, shape, dt))

        def sem(name):
            return ctx.enter_context(nc.semaphore(name))

        w_raw = sb("w_raw", [P, 3, KD, D], F32)
        w_hi = sb("w_hi", [P, 3, KD, D], F32R)
        w_lo = sb("w_lo", [P, 3, KD, D], F32R)
        bv_row = sb("bv_row", [P, D], F32)
        ident = sb("ident", [P, P], F32)
        x_in = sb("x_in", [P, TT, D], F32)
        xn = sb("xn", [P, TT, D], F32)
        c_in = sb("c_in", [P, KD, CH], F32)
        c_hi = sb("c_hi", [P, KD, CH], F32R)
        c_lo = sb("c_lo", [P, KD, CH], F32R)
        t_hi = sb("t_hi", [P, KD, CH], F32R)
        t_lo = sb("t_lo", [P, KD, CH], F32R)
        k_hi = sb("k_hi_s", [P, NG, CH], F32R)
        k_lo = sb("k_lo_s", [P, NG, CH], F32R)
        q_hi = sb("q_hi_s", [P, NG, CH], F32R)
        q_lo = sb("q_lo_s", [P, NG, CH], F32R)
        v_out = sb("v_out", [P, TT, D], F32)
        stats = sb("stats", [P, TT, 6], F32)
        mv = sb("mv", [P, TT, 2], F32)
        ve = sb("ve", [P, TT], F32)
        sd = sb("sd", [P, TT], F32)
        r0 = sb("r0", [P, TT], F32)
        r1 = sb("r1", [P, TT], F32)
        r2 = sb("r2", [P, TT], F32)
        rstd = sb("rstd", [P, TT], F32)
        gate = sb("gate", [P, 1], F32)
        bank = ctx.enter_context(nc.psum_tensor("p1_bank", [P, 8, 512], F32))

        w_in = sem("w_in")
        w_split = sem("w_split")
        x_loaded = sem("x_loaded")
        c_loaded = sem("c_loaded")
        c_hi_done = sem("c_hi_done")
        c_lo_done = sem("c_lo_done")
        chain = sem("chain")
        sd_ready = sem("sd_ready")
        xn_ready = sem("xn_ready")
        filled = sem("filled")
        hi_done = sem("hi_done")
        lo_done = sem("lo_done")
        k_stored = sem("k_stored")
        q_stored = sem("q_stored")
        v_stored = sem("v_stored")

        xr = a.x.rearrange("b s d -> (b s) d").rearrange("(c t p) d -> c p t d", t=TT, p=P)
        cr = a.ctx_t.rearrange("c (k p) s -> c p k s", p=P)
        vr = m.v.rearrange("(c t p) d -> c p t d", t=TT, p=P)

        by_chunk = {n: x.rearrange("g p (c s) -> c p g s", c=NCH) for n, x in
                    (("k_hi", m.k_hi), ("k_lo", m.k_lo), ("q_hi", m.q_hi), ("q_lo", m.q_lo))}

        GPC = 16
        APC = 12
        CHAIN = 8

        with nc.Block() as block:
            @block.sync
            def _(sp):
                for i, w in enumerate((a.wq_t, a.wk_t, a.wv_t)):
                    sp.dma_start(w_raw[:, i], w.rearrange("(k p) n -> p k n", p=P)).then_inc(w_in, 16)
                sp.dma_start(ident[:], a.ident).then_inc(w_in, 16)
                sp.dma_start(bv_row[:], a.bv.unsqueeze(0).broadcast_to([P, D])).then_inc(w_in, 16)
                sp.dma_start(x_in[:], xr[0]).then_inc(x_loaded, 16)
                sp.dma_start(c_in[:], cr[0]).then_inc(c_loaded, 16)

                def body(c, last):
                    cur, nxt = held(sp, c), held(sp, c + 1)
                    x_free, k_done = held(sp, c * TT + TT), held(sp, c * GPC + 8)
                    v_done, q_done = held(sp, c * GPC + 12), held(sp, c * GPC + 16)
                    if not last:
                        sp.wait_ge(xn_ready, x_free)
                        sp.dma_start(x_in[:], xr[nxt]).then_inc(x_loaded, 16)
                        sp.wait_ge(c_lo_done, nxt)
                        sp.dma_start(c_in[:], cr[nxt]).then_inc(c_loaded, 16)
                    sp.wait_ge(lo_done, k_done)
                    sp.dma_start(by_chunk["k_hi"][cur], k_hi[:].bitcast(F32)).then_inc(k_stored, 16)
                    sp.dma_start(by_chunk["k_lo"][cur], k_lo[:].bitcast(F32)).then_inc(k_stored, 16)
                    sp.wait_ge(lo_done, v_done)
                    sp.dma_start(vr[cur], v_out[:]).then_inc(v_stored, 16)
                    sp.wait_ge(lo_done, q_done)
                    sp.dma_start(by_chunk["q_hi"][cur], q_hi[:].bitcast(F32)).then_inc(q_stored, 16)
                    sp.dma_start(by_chunk["q_lo"][cur], q_lo[:].bitcast(F32)).then_inc(q_stored, 16)

                with sp.Fori(0, NCH - 1) as c:
                    body(c, False)
                body(NCH - 1, True)
                sp.wait_ge(k_stored, 32 * NCH)
                sp.wait_ge(v_stored, 16 * NCH)
                sp.wait_ge(q_stored, 32 * NCH)

            @block.scalar
            def _(act):
                act.wait_ge(w_in, 80)
                for i in range(3):
                    act.copy(w_hi[:, i], w_raw[:, i]).then_inc(w_split, 1)

                def next_chunk_sd(c):
                    act.wait_ge(chain, c * CHAIN + 3)
                    act.activation(sd[:], ve[:], ACT.Sqrt).then_inc(sd_ready, 1)

                def next_chunk_hi(c, first):
                    act.wait_ge(c_loaded, 16 * c + 16)
                    if not first:
                        act.wait_ge(filled, (c - 1) * GPC + 12)
                    act.copy(c_hi[:], c_in[:]).then_inc(c_hi_done, 1)

                next_chunk_sd(0)
                next_chunk_hi(0, True)

                def body(c, first, last):
                    for k in range(KD):
                        act.wait_ge(filled, c * GPC + k + 1)
                        act.copy(t_hi[:, k], bank[:, k]).then_inc(hi_done, 1)
                    for g in range(NG):
                        act.wait_ge(filled, c * GPC + 4 + g + 1)
                        if not first and g == 0:
                            act.wait_ge(k_stored, 32 * c)
                        act.copy(k_hi[:, g], bank[:, 4 + g]).then_inc(hi_done, 1)
                    if not last:
                        next_chunk_sd(c + 1)
                        next_chunk_hi(c + 1, False)
                    for g in range(NG):
                        act.wait_ge(filled, c * GPC + 12 + g + 1)
                        if not first and g == 0:
                            act.wait_ge(q_stored, 32 * c)
                        act.copy(q_hi[:, g], bank[:, 4 + g]).then_inc(hi_done, 1)

                body(0, True, False)
                with act.Fori(1, NCH - 1) as c:
                    body(c, False, False)
                body(NCH - 1, False, True)

            @block.vector
            def _(dve):
                def link(c, n, ins):
                    ins.then_inc(chain, 1)
                    dve.wait_ge(chain, c * CHAIN + n)

                def ln_rstd(c, n):
                    dve.wait_ge(sd_ready, c + 1)
                    link(c, n, dve.reciprocal(r0[:], sd[:]))
                    link(c, n + 1, dve.tensor_tensor(r1[:], r0[:], r0[:], ALU.mult))
                    link(c, n + 2, dve.tensor_tensor(r2[:], r1[:], ve[:], ALU.mult))
                    link(c, n + 3, dve.tensor_scalar(r1[:], r2[:], -0.5, 1.5, ALU.mult, ALU.add))
                    link(c, n + 4, dve.tensor_tensor(rstd[:], r0[:], r1[:], ALU.mult))

                def ln_apply(c, t, first):
                    if not first and t == 0:
                        dve.wait_ge(filled, (c - 1) * GPC + 4)
                    dve.tensor_scalar(xn[:, t], x_in[:, t], mv[:, t, 0:1], rstd[:, t:t + 1],
                                      ALU.subtract, ALU.mult).then_inc(xn_ready, 1)

                def ctx_lo(c, first):
                    dve.wait_ge(c_hi_done, c + 1)
                    dve.tensor_tensor(c_lo[:], c_in[:], c_hi[:].bitcast(F32), ALU.subtract).then_inc(c_lo_done, 1)

                def stats_all(c):
                    dve.wait_ge(x_loaded, 16 * c + 16)
                    for t in range(TT):
                        ins = dve.bn_stats(stats[:, t], x_in[:, t])
                    link(c, 1, ins)
                    dve.memset(gate[:], 0.0)
                    for t in range(TT):
                        ins = dve.bn_aggr(mv[:, t], stats[:, t])
                    link(c, 2, ins)
                    link(c, 3, dve.tensor_scalar(ve[:], mv[:, :, 1], EPS, None, ALU.add))

                stats_all(0)
                ln_rstd(0, 4)
                for t in range(TT):
                    ln_apply(0, t, True)
                ctx_lo(0, True)
                dve.wait_ge(w_split, 3)
                for i in range(3):
                    dve.tensor_tensor(w_lo[:, i], w_raw[:, i], w_hi[:, i].bitcast(F32), ALU.subtract).then_inc(w_split, 1)

                def body(c, first, last):
                    for k in range(KD):
                        dve.wait_ge(hi_done, c * APC + k + 1)
                        dve.tensor_tensor(t_lo[:, k], bank[:, k], t_hi[:, k].bitcast(F32),
                                          ALU.subtract).then_inc(lo_done, 1)
                    for g in range(NG):
                        dve.wait_ge(hi_done, c * APC + 4 + g + 1)
                        dve.tensor_tensor(k_lo[:, g], bank[:, 4 + g], k_hi[:, g].bitcast(F32),
                                          ALU.subtract).then_inc(lo_done, 1)
                    if not last:
                        stats_all(c + 1)
                    for t in range(TT):
                        dve.wait_ge(filled, c * GPC + 8 + t + 1)
                        if not first and t == 0:
                            dve.wait_ge(v_stored, 16 * c)
                        dve.tensor_tensor(v_out[:, t], bank[:, t], bv_row[:], ALU.add).then_inc(lo_done, 1)
                        if not last and t == 0:
                            ln_rstd(c + 1, 4)
                        if not last:
                            ln_apply(c + 1, t, False)
                    if not last:
                        ctx_lo(c + 1, False)
                    for g in range(NG):
                        dve.wait_ge(hi_done, c * APC + 8 + g + 1)
                        dve.tensor_tensor(q_lo[:, g], bank[:, 4 + g], q_hi[:, g].bitcast(F32),
                                          ALU.subtract).then_inc(lo_done, 1)

                body(0, True, False)
                with dve.Fori(1, NCH - 1) as c:
                    body(c, False, False)
                body(NCH - 1, False, True)

            @block.tensor
            def _(pe):
                pe.wait_ge(w_in, 80)
                pe.wait_ge(w_split, 6)

                def split_product(out, lhs, rhs):
                    for k in range(KD):
                        (lh, ll), (rh, rl) = lhs(k), rhs(k)
                        pe.matmul(out, lh, rh, start=(k == 0), stop=False)
                        pe.matmul(out, lh, rl, start=False, stop=False)
                        mm = pe.matmul(out, ll, rh, start=False, stop=(k == KD - 1))
                    mm.then_inc(filled, 1)

                def body(c, first):
                    pe.wait_ge(xn_ready, c * TT + TT)
                    for k in range(KD):
                        if not first:
                            pe.wait_ge(lo_done, (c - 1) * GPC + 8 + k + 1)
                        for t in range(TT):
                            mm = pe.transpose(bank[:, k, t * P:(t + 1) * P], xn[:, t, k * P:(k + 1) * P], ident[:])
                        mm.then_inc(filled, 1)
                    pe.wait_ge(c_lo_done, c + 1)
                    for g in range(NG):
                        if not first:
                            pe.wait_ge(lo_done, (c - 1) * GPC + 12 + g + 1)
                        split_product(bank[:, 4 + g],
                                      lambda k: [w[:, 1, k, g * P:(g + 1) * P] for w in (w_hi, w_lo)],
                                      lambda k: [c_hi[:, k], c_lo[:, k]])
                    for t in range(TT):
                        pe.wait_ge(lo_done, c * GPC + t + 1)
                        split_product(bank[:, t],
                                      lambda k: [x[:, k, t * P:(t + 1) * P] for x in (c_hi, c_lo)],
                                      lambda k: [w_hi[:, 2, k], w_lo[:, 2, k]])
                    for g in range(NG):
                        pe.wait_ge(lo_done, c * GPC + 4 + g + 1)
                        split_product(bank[:, 4 + g],
                                      lambda k: [w[:, 0, k, g * P:(g + 1) * P] for w in (w_hi, w_lo)],
                                      lambda k: [t_hi[:, k], t_lo[:, k]])

                body(0, True)
                with pe.Fori(1, NCH) as c:
                    body(c, False)


def attend(nc, a, m):
    NIT = B * NG
    ST = S // P
    SLOTS = 3
    R = 3 * HD
    STEPS = [(sh, j) for sh in range(2) for j in range(4 * (sh + 1))]
    NS = len(STEPS)
    CHUNKS = []
    for h in range(HG):
        for i in range(ST):
            if i >= 4:
                CHUNKS.append((h, i, 0, CH, False))
            t0 = CH * (i // 4)
            CHUNKS.append((h, i, t0, (i + 1) * P - t0, True))
    NC = len(CHUNKS)
    MAX_STEPS = 9
    LOADS = 7 * 16
    RP = 4
    AFTER = {8: 0, 11: 1, 14: 2, 17: 3, 30: 4, 33: 5, 36: 6, 39: 7}

    with ExitStack() as ctx:
        def sb(name, shape, dt):
            return ctx.enter_context(nc.sbuf_tensor(name, shape, dt))

        def sem(name):
            return ctx.enter_context(nc.semaphore(name))

        ks = [sb(f"k_stack{i}", [P, HG, S], F32R) for i in range(SLOTS)]
        qs = [sb(f"q_stack{i}", [P, HG, S], F32R) for i in range(SLOTS)]
        vt = [sb(f"v_tile{i}", [P, ST, P], F32) for i in range(SLOTS)]
        pt = sb("p_t", [P, 2, HG, CH], F32)
        mask_f = sb("mask_f", [P, 4, P], F32)
        mask_ts = sb("mask_ts", [P, 2, P], BF16)
        mask_st = sb("mask_st", [P, 2, P], BF16)
        ident = sb("ident2", [P, P], F32)
        ident_b = sb("ident_b", [P, P], BF16)
        ones = sb("ones", [P, HD], F32)
        mx_a = sb("mx_a", [P, HG * ST], F32)
        mx_b = sb("mx_b", [P, HG * ST], F32)
        mx = sb("mx", [P, HG * ST], F32)
        m_row = sb("m_row", [HG * ST, P], F32R)
        o_sb = sb("o_sb", [P, 2, CH], F32)
        d_sb = sb("d_sb", [P, 2, CH], F32)
        r_sb = sb("r_sb", [P, 2, CH], F32)
        o_n = sb("o_n", [P, 2, CH], F32)
        bank = ctx.enter_context(nc.psum_tensor("p2_bank", [P, 8, 512], F32))
        MX, OB, DB = 4, 6, 7

        const_in = sem("const_in")
        const_ready = sem("const_ready")
        loaded = [sem(f"loaded{i}") for i in range(SLOTS)]
        scored = sem("scored")
        exp_done = sem("exp_done")
        step_done = sem("step_done")
        mx_filled = sem("mx_filled")
        mx_read = sem("mx_read")
        mx_ready = sem("mx_ready")
        mx_turned = sem("mx_turned")
        m_row_ready = sem("m_row_ready")
        m_placed = sem("m_placed")
        o_read = sem("o_read")
        inverted = sem("inverted")
        divided = sem("divided")
        o_stored = [sem(f"o_stored{i}") for i in range(2)]

        def load(eng, it, slot):
            b, g = it // NG, it % NG
            for stack, parts in ((ks[slot], (m.k_hi, m.k_lo, m.k_hi)), (qs[slot], (m.q_hi, m.q_hi, m.q_lo))):
                for r, part in enumerate(parts):
                    src = part.rearrange("g (h p) (b s) -> b g p h s", p=HD, b=B)[b, g]
                    eng.dma_start(stack[r * HD:(r + 1) * HD].bitcast(F32), src).then_inc(loaded[slot], 16)
            src = m.v.rearrange("(b t p) (g n) -> b g p t n", b=B, p=P, g=NG)[b, g]
            eng.dma_start(vt[slot][:], src).then_inc(loaded[slot], 16)

        with nc.Block() as block:
            @block.sync
            def _(sp):
                sp.dma_start(mask_f[:, 0:2], a.mask_ts.rearrange("v t s -> t v s")).then_inc(const_in, 16)
                sp.dma_start(mask_f[:, 2:4], a.mask_st.rearrange("v s t -> s v t")).then_inc(const_in, 16)
                sp.dma_start(ident[:], a.ident).then_inc(const_in, 16)
                load(sp, 0, 0)
                load(sp, 1, 1)

                def place_max(it, slot):
                    sp.wait_ge(m_row_ready, it)
                    sp.dma_start(qs[slot][R:R + 1].rearrange("p h s -> p (h s)").bitcast(F32),
                                 m_row[:].bitcast(F32)).then_inc(m_placed, 16)

                def store(it, half, n):
                    sp.wait_ge(divided, n)
                    sp.dma_start(m.o.rearrange("g p (b s) -> b g p s", b=B)[it // NG, it % NG][:, half * CH:(half + 1) * CH],
                                 o_n[:, half]).then_inc(o_stored[half], 16)

                def body(it, slot, first, last, more):
                    cur, prev, nxt = held(sp, it), held(sp, it - 1), held(sp, it + 1)
                    ahead = held(sp, it + 2)
                    steps, two_it = held(sp, it * NS), held(sp, it * 2)
                    this_half, place_at = held(sp, it * 2 + 1), held(sp, it + 2)
                    if more:
                        if not first:
                            sp.wait_ge(step_done, steps)
                        load(sp, ahead, (slot + 2) % SLOTS)
                    if not first:
                        store(prev, 1, two_it)
                    store(cur, 0, this_half)
                    if not last:
                        place_max(place_at, (slot + 1) % SLOTS)

                place_max(1, 0)
                body(0, 0, True, False, True)
                with sp.Fori(0, (NIT - 4) // SLOTS) as g:
                    for u in range(SLOTS):
                        body(g * SLOTS + (1 + u), (1 + u) % SLOTS, False, False, True)
                for it in range(NIT - 3, NIT):
                    body(it, it % SLOTS, False, it == NIT - 1, it + 2 < NIT)
                store(NIT - 1, 1, 2 * NIT)
                for half in range(2):
                    sp.wait_ge(o_stored[half], 16 * NIT)

            @block.gpsimd
            def _(pool):
                pool.wait_ge(const_in, 48)
                pool.tensor_copy(ident_b[:], ident[:]).then_inc(const_ready, 1)
                pool.tensor_copy(mask_ts[:], mask_f[:, 0:2]).then_inc(const_ready, 1)
                pool.tensor_copy(mask_st[:], mask_f[:, 2:4]).then_inc(const_ready, 1)

                def body(it, first):
                    for half in range(2):
                        pool.wait_ge(inverted, (it * 2 + half) * RP + RP)
                        if not first:
                            pool.wait_ge(o_stored[half], it * 16)
                        pool.tensor_tensor(o_n[:, half], o_sb[:, half], r_sb[:, half], ALU.mult).then_inc(divided, 1)

                body(0, True)
                with pool.Fori(1, NIT) as it:
                    body(it, False)

            @block.vector
            def _(dve):
                dve.memset(ones[:], 1.0).then_inc(const_ready, 1)
                dve.memset(mx_b[:], -3e38).then_inc(const_ready, 1)
                for i in range(SLOTS):
                    dve.memset(ks[i][R:R + 1].bitcast(F32), 1.0).then_inc(const_ready, 1)
                dve.wait_ge(const_ready, 8)

                def invert(hf, half, q, first):
                    if q == 0:
                        dve.wait_ge(o_read, hf * 2 + 2)
                        if not first:
                            dve.wait_ge(divided, hf - 1)
                    dve.reciprocal(r_sb[:, half, q * P:(q + 1) * P], d_sb[:, half, q * P:(q + 1) * P]
                                   ).then_inc(inverted, 1)

                def maxima(it, first, older, older_first):
                    for n, (h, i, t0, w, diag) in enumerate(CHUNKS):
                        if n == 0 and not first:
                            dve.wait_ge(mx_ready, it)
                        dve.wait_ge(mx_filled, it * NC + n + 1)
                        to = mx_a if t0 == 0 else mx_b
                        dve.tensor_reduce(to[:, h * ST + i:h * ST + i + 1], bank[:, MX + n % 2, 0:w], AX.X,
                                          ALU.max).then_inc(mx_read, 1)
                        if n in AFTER and not first:
                            q = AFTER[n]
                            if q < RP and older:
                                invert(it * 2 - 3, 1, q, older_first)
                            if q >= RP:
                                invert(it * 2 - 2, 0, q - RP, not older)
                    dve.wait_ge(mx_read, it * NC + NC)
                    if not first:
                        dve.wait_ge(mx_turned, it)
                    dve.tensor_tensor(mx[:], mx_a[:], mx_b[:], ALU.max).then_inc(mx_ready, 1)

                maxima(0, True, False, False)
                maxima(1, False, False, False)
                maxima(2, False, True, True)
                with dve.Fori(3, NIT) as it:
                    maxima(it, False, True, False)
                for hf in range(2 * NIT - 3, 2 * NIT):
                    for q in range(RP):
                        invert(hf, hf % 2, q, False)

            @block.scalar
            def _(act):
                def negate(it, first):
                    act.wait_ge(mx_turned, it + 1)
                    if not first:
                        act.wait_ge(m_placed, it * 16)
                    act.activation(m_row[:], bank[0:HG * ST, MX, 0:P], ACT.Copy, scale=-1.0).then_inc(m_row_ready, 1)

                def take(it, half, first):
                    act.wait_ge(step_done, it * NS + (4 if half == 0 else NS))
                    if not first:
                        act.wait_ge(divided, it * 2 + half - 1)
                    act.copy(o_sb[:, half], bank[:, OB]).then_inc(o_read, 1)
                    act.copy(d_sb[:, half], bank[:, DB]).then_inc(o_read, 1)

                def body(it, first, last):
                    for k, (sh, j) in enumerate(STEPS):
                        w = CH * (sh + 1) - max(CH * sh, P * j)
                        for h in range(HG):
                            act.wait_ge(scored, (it * NS + k) * HG + h + 1)
                            if h == 0 and not (first and k < 2):
                                act.wait_ge(step_done, it * NS + k - 1)
                            act.activation(pt[:, k % 2, h, 0:w], bank[:, h, 0:w], ACT.Exp,
                                           scale=SCALE).then_inc(exp_done, 1)
                        if k == 0 and not first:
                            take(it - 1, 1, False) if not isinstance(it, int) or it > 1 else take(0, 1, True)
                        if k == 4:
                            take(it, 0, first)
                        if k == MAX_STEPS and not last:
                            negate(it + 1, False)

                negate(0, True)
                body(0, True, False)
                body(1, False, False)
                with act.Fori(2, NIT - 1) as it:
                    body(it, False, False)
                body(NIT - 1, False, True)
                take(NIT - 1, 1, False)

            @block.tensor
            def _(pe):
                pe.wait_ge(const_ready, 8)

                def chunk(it, n, slot, first):
                    h, i, t0, w, diag = CHUNKS[n]
                    if n == 0 and not first:
                        pe.wait_ge(m_row_ready, it)
                    if not (first and n < 2):
                        pe.wait_ge(mx_read, it * NC + n - 1)
                    out = bank[:, MX + n % 2, 0:w]
                    mm = pe.matmul(out, qs[slot][0:R, h, i * P:(i + 1) * P], ks[slot][0:R, h, t0:t0 + w],
                                   start=True, stop=not diag)
                    if diag:
                        mm = pe.matmul(bank[:, MX + n % 2, w - P:w], ident_b[:], mask_st[:, 1 if i == 0 else 0],
                                       start=False, stop=True)
                    mm.then_inc(mx_filled, 1)

                def turn(it):
                    pe.wait_ge(mx_ready, it + 1)
                    pe.transpose(bank[0:HG * ST, MX, 0:P], mx[:], ident[:]).then_inc(mx_turned, 1)

                def scores(it, k, slot, first, heads):
                    sh, j = STEPS[k]
                    s0 = max(CH * sh, P * j)
                    w = CH * (sh + 1) - s0
                    diag = P * j >= CH * sh
                    if k == 0 and heads[0] == 0:
                        pe.wait_ge(m_placed, it * 16 + 16)
                    for h in heads:
                        if not (first and k == 0):
                            pe.wait_ge(exp_done, (it * NS + k - 1) * HG + h + 1)
                        mm = pe.matmul(bank[:, h, 0:w], ks[slot][0:R + 1, h, j * P:(j + 1) * P],
                                       qs[slot][0:R + 1, h, s0:s0 + w], start=True, stop=not diag)
                        if diag:
                            mm = pe.matmul(bank[:, h, 0:P], ident_b[:], mask_ts[:, 1 if j == 0 else 0],
                                           start=False, stop=True)
                        mm.then_inc(scored, 1)

                def values(it, k, slot, first):
                    sh, j = STEPS[k]
                    s0 = max(CH * sh, P * j)
                    w = CH * (sh + 1) - s0
                    c0 = s0 - CH * sh
                    if j == 0 and not (first and sh == 0):
                        pe.wait_ge(o_read, (it * 2 + sh) * 2)
                    for h in range(HG):
                        pe.wait_ge(exp_done, (it * NS + k) * HG + h + 1)
                        pe.matmul(bank[h * HD:(h + 1) * HD, OB, c0:c0 + w], vt[slot][:, j, h * HD:(h + 1) * HD],
                                  pt[:, k % 2, h, 0:w], start=(j == 0), stop=(j == 4 * sh + 3),
                                  tile_position=(0, h * HD), skip_group_check=True)

                def sums(k):
                    sh, j = STEPS[k]
                    c0 = max(0, P * j - CH * sh)
                    w = CH - c0
                    for h in range(HG):
                        mm = pe.matmul(bank[h * HD:(h + 1) * HD, DB, c0:c0 + w], ones[:],
                                       pt[:, k % 2, h, 0:w], start=(j == 0), stop=(j == 4 * sh + 3),
                                       tile_position=(0, h * HD), skip_group_check=True)
                    mm.then_inc(step_done, 1)

                def body(it, slot, first, last, load_count):
                    nslot = (slot + 1) % SLOTS
                    for k in range(NS):
                        due = []
                        if not last:
                            if k == 0:
                                pe.wait_ge(loaded[nslot], load_count)
                            if k < MAX_STEPS:
                                due = list(range(NC * k // MAX_STEPS, NC * (k + 1) // MAX_STEPS))

                        def some(parts_left):
                            for _ in range(-(-len(due) // parts_left)):
                                chunk(it + 1, due.pop(0), nslot, False)

                        nxt = (it, k + 1, slot) if k < NS - 1 else None if last else (it + 1, 0, nslot)
                        if nxt:
                            scores(*nxt, False, (0, 1))
                        some(4)
                        if nxt:
                            scores(*nxt, False, (2, 3))
                        some(3)
                        values(it, k, slot, first)
                        some(2)
                        sums(k)
                        some(1)
                        if k == MAX_STEPS and not last:
                            turn(it + 1)

                pe.wait_ge(loaded[0], LOADS)
                for n in range(NC):
                    chunk(0, n, 0, True)
                turn(0)
                scores(0, 0, 0, True, range(HG))
                body(0, 0, True, False, LOADS)
                with pe.Fori(0, (NIT - 4) // SLOTS) as g:
                    for u in range(SLOTS):
                        body(g * SLOTS + (1 + u), (1 + u) % SLOTS, False, False,
                             (g + (2 + u) // SLOTS + 1) * LOADS)
                for it in range(NIT - 3, NIT):
                    body(it, it % SLOTS, False, it == NIT - 1, ((it + 1) // SLOTS + 1) * LOADS)


def dispatch(nc, a, m, inner):
    NT = S // P
    GB = S // GT
    GQ = P // GT
    CHAIN = 7

    with ExitStack() as ctx:
        def sb(name, shape, dt):
            return ctx.enter_context(nc.sbuf_tensor(name, shape, dt))

        def sem(name):
            return ctx.enter_context(nc.semaphore(name))

        f1 = sb("f1_sb", [P, KD, NE * F], F32)
        disp = sb("disp_t", [P, KD, NE, GB], F32)
        wo_raw = disp[:, 0, 0:NE // 2].rearrange("p e g -> p (e g)").rearrange("p (k n) -> p k n", k=KD)
        wo_hi = sb("wo_hi", [P, KD, D], F32R)
        wo_lo = sb("wo_lo", [P, KD, D], F32R)
        ctl = sb("ctl", [P, KD, NE], F32)
        bo_row = sb("bo_row", [P, D], F32)
        bias = sb("bias_sb", [P, E4], F32)
        ident = sb("ident3", [P, P], F32)
        tie = sb("tie", [P, GT], F32)
        blocks = sb("blocks3", [P, GQ], F32)
        o_raw = sb("o_raw", [P, 2, KD, P], F32)
        o_hi = sb("o_hi", [P, 2, KD, P], F32R)
        o_lo = sb("o_lo", [P, 2, KD, P], F32R)
        xb = sb("xb", [P, 2, D], F32)
        x2 = sb("x2", [P, 2, D], F32)
        xn = sb("xn3", [P, D], F32)
        xn_hi = sb("xn_hi", [P, 2, D], F32R)
        xn_lo = sb("xn_lo", [P, 2, D], F32R)
        xn_t = sb("xn_t", [P, 2, KD, P], F32)
        stats = sb("stats3", [P, 6], F32)
        mv = sb("mv3", [P, 2], F32)
        ve = sb("ve3", [P, 1], F32)
        sd = sb("sd3", [P, 1], F32)
        r0 = sb("r03", [P, 1], F32)
        r1 = sb("r13", [P, 1], F32)
        rstd = sb("rstd3", [P, 1], F32)
        gate = sb("gate3", [P, 1], F32)
        logits = sb("logits", [P, P], F32)
        best = sb("best", [P, GQ], F32)
        pick_t = sb("pick_t", [P, 2, P], F32)
        pick = sb("pick", [P, 2, GQ, NE], F32R)
        bank = ctx.enter_context(nc.psum_tensor("p3_bank", [P, 8, 512], F32))
        A, TB, LB, DB, EB, FB = 0, 2, 3, 4, 5, (7, 4)

        const_in = sem("c3_in")
        f1_in = sem("f1_in")
        wo_split = sem("wo_split")
        o_loaded = [sem(f"o_loaded{i}") for i in range(2)]
        x_loaded = [sem(f"x3_loaded{i}") for i in range(2)]
        x2_stored = [sem(f"x2_stored{i}") for i in range(2)]
        pick_stored = [sem(f"pick_stored{i}") for i in range(2)]
        o_hi_done = sem("o_hi_done")
        o_lo_done = sem("o_lo_done")
        xb_done = sem("xb_done")
        attended = sem("attended")
        x2_done = sem("x2_done")
        chain = sem("chain3")
        sd_done = sem("sd3_done")
        xn_done = sem("xn3_done")
        xn_hi_done = sem("xn3_hi_done")
        xn_lo_done = sem("xn3_lo_done")
        turned = sem("turned")
        xn_t_done = sem("xn_t_done")
        routed = sem("routed")
        tie_done = sem("tie_done")
        best_done = sem("best_done")
        pick_t_done = sem("pick_t_done")
        pick_turned = sem("pick_turned")
        pick_done = sem("pick_done")
        gathered = sem("gathered")
        taken_a = sem("taken_a")
        taken_v = sem("taken_v")
        hidden = sem("hidden")
        biased = sem("biased")
        relued = sem("relued")

        o_src = m.o.rearrange("g p (i s) -> i p g s", s=P)
        x_src = a.x.rearrange("b s d -> (b s) d").rearrange("(i p) d -> i p d", p=P)
        x2_dst = m.x2.rearrange("(i p) d -> i p d", p=P)

        with nc.Block() as block:
            @block.sync
            def _(sp):
                for dst, src in ((wo_raw, a.wo_t.rearrange("(k p) n -> p k n", p=P)),
                                 (ident[:], a.ident), (ctl[:], a.controller.rearrange("(k p) n -> p k n", p=P)),
                                 (bo_row[:], a.bo.unsqueeze(0).broadcast_to([P, D])),
                                 (tie[:], a.tie_row.unsqueeze(0).broadcast_to([P, GT])),
                                 (blocks[:], a.block_cols), (bias[:], a.bias_col)):
                    sp.dma_start(dst, src).then_inc(const_in, 16)

                def load(i, n, first):
                    tile, free = held(sp, i), held(sp, i - 1)
                    if not (first and n < 2):
                        sp.wait_ge(o_lo_done, free)
                    sp.dma_start(o_raw[:, n % 2], o_src[tile]).then_inc(o_loaded[n % 2], 16)
                    if not (first and n < 2):
                        sp.wait_ge(x2_done, free)
                    sp.dma_start(xb[:, n % 2], x_src[tile]).then_inc(x_loaded[n % 2], 16)

                load(0, 0, True)
                load(1, 1, True)
                sp.dma_start(f1[:], a.f1.rearrange("(k p) n -> p k n", p=P)).then_inc(f1_in, 16)
                for n in range(2, NT):
                    load(n, n, True)
                with sp.Fori(1, B) as b:
                    for n in range(NT):
                        load(b * NT + n, n, False)

            def stages(b, n):
                known = isinstance(b, int)
                return (not (known and b == B), not (known and b == 0 and n < 1) and not (known and b == B and n > 0),
                        not (known and b == 0 and n < 2))

            @block.gpsimd
            def _(pool):
                pool.wait_ge(const_in, 16 * 7)

                def o_part(b, n):
                    pool.wait_ge(o_hi_done, b * NT + n + 1)
                    pool.tensor_tensor(o_lo[:, n % 2], o_raw[:, n % 2], o_hi[:, n % 2].bitcast(F32),
                                       ALU.subtract).then_inc(o_lo_done, 1)

                def x_part(b, n):
                    pool.wait_ge(x_loaded[n % 2], (b * (NT // 2) + n // 2) * 16 + 16)
                    pool.tensor_tensor(xb[:, n % 2], xb[:, n % 2], bo_row[:], ALU.add).then_inc(xb_done, 1)

                def body(b, first, last):
                    for n in range(NT):
                        i = b * NT + n
                        if n < NT - 1 or not last:
                            o_part(b + (n + 1) // NT, (n + 1) % NT)
                            x_part(b + (n + 1) // NT, (n + 1) % NT)
                        pool.wait_ge(xn_hi_done, i + 1)
                        if not (first and n < 2):
                            pool.wait_ge(gathered, (i - 1) * KD)
                        pool.tensor_tensor(xn_lo[:, n % 2], xn[:], xn_hi[:, n % 2].bitcast(F32),
                                           ALU.subtract).then_inc(xn_lo_done, 1)

                o_part(0, 0)
                x_part(0, 0)
                body(0, True, False)
                with pool.Fori(1, B - 1) as b:
                    body(b, False, False)
                body(B - 1, False, True)

            @block.scalar
            def _(act):
                act.wait_ge(const_in, 16 * 7)
                act.copy(wo_hi[:], wo_raw).then_inc(wo_split, 1)

                def o_part(b, n, first):
                    act.wait_ge(o_loaded[n % 2], (b * (NT // 2) + n // 2) * 16 + 16)
                    if not (first and n < 2):
                        act.wait_ge(attended, b * NT + n - 1)
                    act.copy(o_hi[:, n % 2], o_raw[:, n % 2]).then_inc(o_hi_done, 1)

                def take(b, n, k):
                    act.wait_ge(gathered, (b * NT + n - 2) * KD + k + 1)
                    if n == 2 and k == 0 and not (isinstance(b, int) and b == 0):
                        act.wait_ge(hidden, b * 2)
                    to = (n - 2) % NT
                    act.copy(disp[:, k, :, to * GQ:(to + 1) * GQ].rearrange("p e g -> p g e"),
                             bank[:, EB + k % 2].rearrange("p (g e) -> p g e", g=GQ)).then_inc(taken_a, 1)

                def slot(b, n, first, last):
                    i = b * NT + n
                    head, middle, tail = stages(b, n)
                    if head and not (last and n == NT - 1):
                        o_part(b + (n + 1) // NT, (n + 1) % NT, first and n < 1)
                    if middle:
                        act.wait_ge(turned, i)
                        if not (first and n < 3):
                            act.wait_ge(routed, i - 2)
                        act.copy(xn_t[:, (n - 1) % 2], bank[:, TB]).then_inc(xn_t_done, 1)
                    if tail:
                        take(b, n, 0)
                    if head:
                        act.wait_ge(chain, i * CHAIN + 3)
                        act.activation(sd[:], ve[:], ACT.Sqrt).then_inc(sd_done, 1)
                    if tail:
                        take(b, n, 2)
                        take(b, n, 3)
                        act.dma_start(m.pick[i - 2], pick_t[:, n % 2]).then_inc(pick_stored[n % 2], 16)
                    if head:
                        act.dma_start(x2_dst[i], x2[:, n % 2]).then_inc(x2_stored[n % 2], 16)
                        act.wait_ge(xn_done, i + 1)
                        if not (first and n < 2):
                            act.wait_ge(gathered, (i - 1) * KD)
                        act.copy(xn_hi[:, n % 2], xn[:]).then_inc(xn_hi_done, 1)

                o_part(0, 0, True)
                for n in range(NT):
                    slot(0, n, True, False)
                with act.Fori(1, B - 1) as b:
                    for n in range(NT):
                        slot(b, n, False, False)
                for n in range(NT):
                    slot(B - 1, n, False, True)
                for n in range(2):
                    slot(B, n, False, True)
                for u in range(2):
                    act.wait_ge(x2_stored[u], 16 * B * NT // 2)
                    act.wait_ge(pick_stored[u], 16 * B * NT // 2)

            @block.vector
            def _(dve):
                dve.wait_ge(const_in, 16 * 7)
                dve.wait_ge(wo_split, 1)
                dve.tensor_tensor(wo_lo[:], wo_raw, wo_hi[:].bitcast(F32), ALU.subtract).then_inc(wo_split, 1)

                def link(i, n, ins):
                    ins.then_inc(chain, 1)
                    dve.wait_ge(chain, i * CHAIN + n)

                grouped = "p (g t) -> p g t"

                def choose(b, i, n, first):
                    dve.wait_ge(routed, i - 1)
                    if not (first and n == 2):
                        dve.wait_ge(pick_t_done, i - 2)
                    dve.tensor_tensor(logits[:].rearrange(grouped, g=GQ),
                                      bank[:, LB, 0:P].rearrange(grouped, g=GQ),
                                      tie[:].unsqueeze(1).broadcast_to([P, GQ, GT]),
                                      ALU.add).then_inc(tie_done, 1)
                    dve.wait_ge(tie_done, i - 1)
                    dve.tensor_reduce(best[:], logits[:].rearrange(grouped, g=GQ), AX.X,
                                      ALU.max).then_inc(best_done, 1)
                    if not (first and n < 4):
                        dve.wait_ge(pick_stored[n % 2], (b * (NT // 2) + (n - 2) // 2) * 16)
                        dve.wait_ge(pick_turned, i - 3)
                    dve.wait_ge(best_done, i - 1)
                    dve.tensor_tensor(pick_t[:, n % 2].rearrange(grouped, g=GQ),
                                      logits[:].rearrange(grouped, g=GQ),
                                      best[:].unsqueeze(2).broadcast_to([P, GQ, GT]),
                                      ALU.is_equal).then_inc(pick_t_done, 1)
                    dve.wait_ge(pick_turned, i - 1)
                    if not (first and n < 4):
                        dve.wait_ge(gathered, (i - 3) * KD)
                    dve.tensor_tensor(pick[:, n % 2],
                                      bank[:, DB, 0:NE].unsqueeze(1).broadcast_to([P, GQ, NE]),
                                      blocks[:].unsqueeze(2).broadcast_to([P, GQ, NE]),
                                      ALU.mult).then_inc(pick_done, 1)

                def slot(b, n, first):
                    i = b * NT + n
                    head, _, tail = stages(b, n)
                    if tail:
                        choose(b, i, n, first)
                    if head:
                        dve.wait_ge(attended, i + 1)
                        dve.wait_ge(xb_done, i + 1)
                        if not (first and n < 2):
                            dve.wait_ge(x2_stored[n % 2], (b * (NT // 2) + n // 2) * 16)
                        dve.tensor_tensor(x2[:, n % 2], bank[:, A + n % 2], xb[:, n % 2],
                                          ALU.add).then_inc(x2_done, 1)
                        dve.wait_ge(x2_done, i + 1)
                        link(i, 1, dve.bn_stats(stats[:], x2[:, n % 2]))
                        dve.memset(gate[:], 0.0)
                        link(i, 2, dve.bn_aggr(mv[:], stats[:]))
                        dve.tensor_scalar(ve[:], mv[:, 1:2], EPS, None, ALU.add).then_inc(chain, 1)
                    if tail:
                        dve.wait_ge(gathered, (i - 2) * KD + 2)
                        to = (n - 2) % NT
                        dve.tensor_copy(disp[:, 1, :, to * GQ:(to + 1) * GQ].rearrange("p e g -> p g e"),
                                        bank[:, EB + 1].rearrange("p (g e) -> p g e", g=GQ)).then_inc(taken_v, 1)
                    if head:
                        dve.wait_ge(sd_done, i + 1)
                        link(i, 4, dve.reciprocal(r0[:], sd[:]))
                        link(i, 5, dve.scalar_tensor_tensor(r1[:], r0[:], r0[:, 0:1], ve[:], ALU.mult, ALU.mult))
                        link(i, 6, dve.tensor_scalar(r1[:], r1[:], -0.5, 1.5, ALU.mult, ALU.add))
                        link(i, 7, dve.tensor_tensor(rstd[:], r0[:], r1[:], ALU.mult))
                        if not (first and n < 1):
                            dve.wait_ge(xn_lo_done, i)
                            dve.wait_ge(turned, i)
                        dve.tensor_scalar(xn[:], x2[:, n % 2], mv[:, 0:1], rstd[:], ALU.subtract,
                                          ALU.mult).then_inc(xn_done, 1)
                    if n == 1 and not first:
                        layer_one(b)

                def layer_one(b):
                    for half in range(2):
                        es = slice(half * (E4 // 2), (half + 1) * (E4 // 2))
                        dve.wait_ge(hidden, b * 2 + half - 1)
                        to = inner[:, es, :].rearrange("p e (b g) -> p b e g", b=B)[:, b - 1]
                        dve.tensor_tensor(to, bank[:, FB[half]].rearrange("p (e g) -> p e g", g=GB),
                                          bias[:, es].unsqueeze(2).broadcast_to([P, E4 // 2, GB]),
                                          ALU.add).then_inc(biased, 1)
                        dve.wait_ge(biased, b * 2 + half - 1)
                        dve.tensor_scalar(to, to, 0.0, None, ALU.max).then_inc(relued, 1)

                for n in range(NT):
                    slot(0, n, True)
                with dve.Fori(1, B) as b:
                    for n in range(NT):
                        slot(b, n, False)
                for n in range(2):
                    slot(B, n, False)

            @block.tensor
            def _(pe):
                pe.wait_ge(wo_split, 2)

                def project_out(n, ks):
                    for k in ks:
                        oh, ol = o_hi[:, n % 2, k], o_lo[:, n % 2, k]
                        pe.matmul(bank[:, A + n % 2], oh, wo_hi[:, k], start=(k == 0), stop=False)
                        pe.matmul(bank[:, A + n % 2], oh, wo_lo[:, k], start=False, stop=False)
                        mm = pe.matmul(bank[:, A + n % 2], ol, wo_hi[:, k], start=False, stop=(k == KD - 1))
                    return mm

                def gather(i, n, first, ks):
                    for k in ks:
                        oldest = first and n == 2
                        if k == 0 and not oldest:
                            pe.wait_ge(taken_a, (i - 2) * 3 - 1)
                        if k == 1 and not oldest:
                            pe.wait_ge(taken_a, (i - 2) * 3)
                        if k == 2:
                            pe.wait_ge(taken_a, (i - 2) * 3 + 1)
                        if k == 3:
                            pe.wait_ge(taken_v, i - 1)
                        out = bank[:, EB + k % 2]
                        rhs = pick[:, n % 2].rearrange("p g e -> p (g e)")
                        pe.matmul(out, xn_hi[:, n % 2, k * P:(k + 1) * P], rhs, start=True, stop=False)
                        pe.matmul(out, xn_lo[:, n % 2, k * P:(k + 1) * P], rhs, start=False,
                                  stop=True).then_inc(gathered, 1)

                def slot(b, n, first):
                    i = b * NT + n
                    head, middle, tail = stages(b, n)
                    if head:
                        pe.wait_ge(o_lo_done, i + 1)
                        if not (first and n < 2):
                            pe.wait_ge(x2_done, i - 1)
                        project_out(n, range(0, KD // 2))
                    if tail:
                        pe.wait_ge(pick_t_done, i - 1)
                        if n == 2 and not first:
                            pe.wait_ge(biased, b * 2)
                        if not (first and n == 2):
                            pe.wait_ge(pick_done, i - 2)
                        pe.transpose(bank[:, DB, 0:P], pick_t[:, n % 2], ident[:]).then_inc(pick_turned, 1)
                    if head:
                        project_out(n, range(KD // 2, KD)).then_inc(attended, 1)
                    if middle:
                        pe.wait_ge(xn_done, i)
                        if not (first and n == 1):
                            pe.wait_ge(xn_t_done, i - 1)
                        for k in range(KD):
                            mm = pe.transpose(bank[:, TB, k * P:(k + 1) * P], xn[:, k * P:(k + 1) * P], ident[:])
                        mm.then_inc(turned, 1)
                    if tail:
                        pe.wait_ge(xn_lo_done, i - 1)
                        pe.wait_ge(pick_done, i - 1)
                        gather(i, n, first, (0, 1))
                    if middle:
                        pe.wait_ge(xn_t_done, i)
                        if not (first and n == 1):
                            pe.wait_ge(tie_done, i - 1)
                        for k in range(KD):
                            mm = pe.matmul(bank[:, LB, 0:P], ctl[:, k], xn_t[:, (n - 1) % 2, k],
                                           start=(k == 0), stop=(k == KD - 1))
                        mm.then_inc(routed, 1)
                    if tail:
                        gather(i, n, first, (2, 3))
                    if n == 1 and not first:
                        layer_one(b)

                def layer_one(b):
                    pe.wait_ge(f1_in, 16)
                    pe.wait_ge(taken_a, b * NT * 3)
                    pe.wait_ge(taken_v, b * NT)
                    for half in range(2):
                        for e in range(E4 // 2):
                            for k in range(KD):
                                for q in range(4):
                                    es = (half * (E4 // 2) + e) * 4 + q
                                    mm = pe.matmul(bank[q * F:(q + 1) * F, FB[half], e * GB:(e + 1) * GB],
                                                   f1[:, k, es * F:(es + 1) * F], disp[:, k, es],
                                                   start=(k == 0), stop=(k == KD - 1), tile_position=(0, q * F),
                                                   skip_group_check=True)
                        mm.then_inc(hidden, 1)

                for n in range(NT):
                    slot(0, n, True)
                with pe.Fori(1, B) as b:
                    for n in range(NT):
                        slot(b, n, False)
                for n in range(2):
                    slot(B, n, False)


def expand(nc, a, m, inner):
    with ExitStack() as ctx:
        def sb(name, shape, dt):
            return ctx.enter_context(nc.sbuf_tensor(name, shape, dt))

        def sem(name):
            return ctx.enter_context(nc.semaphore(name))

        in_hi = sb("in_hi", [P, E4, NGR], F32R)
        in_lo = sb("in_lo", [P, E4, NGR], F32R)
        blocks = sb("blocks4", [P, 4], F32)
        raw = sb("f2_raw", [P, 2, D], F32)
        w_hi = sb("f2_hi", [P, 2, D], F32R)
        w_lo = sb("f2_lo", [P, 2, D], F32R)
        d_hi = sb("d_hi", [P, 2, 4, NGR], F32R)
        d_lo = sb("d_lo", [P, 2, 4, NGR], F32R)
        y = sb("y_sb", [P, 2, 4, D], F32)
        bank = ctx.enter_context(nc.psum_tensor("p4_bank", [P, 8, 512], F32))

        c_in = sem("c4_in")
        in_split = sem("in_split")
        loaded = [sem(f"f2_loaded{i}") for i in range(2)]
        w_hi_done = sem("f2_hi_done")
        w_lo_done = sem("f2_lo_done")
        d_hi_done = sem("d_hi_done")
        d_lo_done = sem("d_lo_done")
        made = sem("y_made")
        taken_a = sem("y_taken_a")
        taken_v = sem("y_taken_v")
        stored = [sem(f"y_stored{i}") for i in range(2)]

        src = a.f2.rearrange("(e p) d -> e p d", p=P)
        dst = m.y.rearrange("g (e q) d -> e g q d", q=4)

        with nc.Block() as block:
            @block.sync
            def _(sp):
                sp.dma_start(blocks[:], a.block_cols).then_inc(c_in, 16)
                for u in range(2):
                    sp.dma_start(raw[:, u], src[u]).then_inc(loaded[u], 16)

                def body(j, more):
                    for u in range(2):
                        e, ahead = held(sp, j * 2 + u), held(sp, j * 2 + u + 2)
                        split, done = held(sp, j * 2 + u + 1), held(sp, (j * 2 + u + 1) * 2)
                        if more:
                            sp.wait_ge(w_lo_done, split)
                            sp.dma_start(raw[:, u], src[ahead]).then_inc(loaded[u], 16)
                        sp.wait_ge(taken_a, done)
                        sp.wait_ge(taken_v, done)
                        sp.dma_start(dst[e], y[:, u]).then_inc(stored[u], 16)

                with sp.Fori(0, E4 // 2 - 1) as j:
                    body(j, True)
                body(E4 // 2 - 1, False)
                for u in range(2):
                    sp.wait_ge(stored[u], 16 * E4 // 2)

            @block.gpsimd
            def _(pool):
                pool.wait_ge(in_split, 2)

                def body(j, first):
                    for u in range(2):
                        if not first:
                            pool.wait_ge(made, (j * 2 + u - 1) * 4)
                        pool.tensor_tensor(d_lo[:, u],
                                           in_lo[:, j * 2 + u].bitcast(F32).unsqueeze(1).broadcast_to([P, 4, NGR]),
                                           blocks[:].unsqueeze(2).broadcast_to([P, 4, NGR]),
                                           ALU.mult).then_inc(d_lo_done, 1)

                body(0, True)
                with pool.Fori(1, E4 // 2) as j:
                    body(j, False)

            @block.scalar
            def _(act):
                act.copy(in_hi[:], inner[:]).then_inc(in_split, 1)

                def split(e, u, more, first):
                    act.wait_ge(loaded[u], more)
                    if not first:
                        act.wait_ge(made, (e - 1) * 4)
                    act.copy(w_hi[:, u], raw[:, u]).then_inc(w_hi_done, 1)

                def body(j, first, last):
                    for u in range(2):
                        e = j * 2 + u
                        if not (last and u == 1):
                            split(e + 1, (u + 1) % 2, (j + (u + 1) // 2) * 16 + 16, first and u == 0)
                        for q in (0, 1):
                            act.wait_ge(made, e * 4 + q + 1)
                            if not first and q == 0:
                                act.wait_ge(stored[u], j * 16)
                            act.copy(y[:, u, q], bank[:, u * 4 + q]).then_inc(taken_a, 1)

                split(0, 0, 16, True)
                body(0, True, False)
                with act.Fori(1, E4 // 2 - 1) as j:
                    body(j, False, False)
                body(E4 // 2 - 1, False, True)

            @block.vector
            def _(dve):
                dve.wait_ge(c_in, 16)
                dve.wait_ge(in_split, 1)
                dve.tensor_tensor(in_lo[:], inner[:], in_hi[:].bitcast(F32), ALU.subtract).then_inc(in_split, 1)

                def prepare(e, u, first):
                    dve.wait_ge(w_hi_done, e + 1)
                    dve.tensor_tensor(w_lo[:, u], raw[:, u], w_hi[:, u].bitcast(F32), ALU.subtract
                                      ).then_inc(w_lo_done, 1)
                    if not first:
                        dve.wait_ge(made, (e - 1) * 4)
                    dve.tensor_tensor(d_hi[:, u], in_hi[:, e].bitcast(F32).unsqueeze(1).broadcast_to([P, 4, NGR]),
                                      blocks[:].unsqueeze(2).broadcast_to([P, 4, NGR]),
                                      ALU.mult).then_inc(d_hi_done, 1)

                def body(j, first, last):
                    for u in range(2):
                        e = j * 2 + u
                        if not (last and u == 1):
                            prepare(e + 1, (u + 1) % 2, first and u == 0)
                        for q in (2, 3):
                            dve.wait_ge(made, e * 4 + q + 1)
                            if not first and q == 2:
                                dve.wait_ge(stored[u], j * 16)
                            dve.tensor_copy(y[:, u, q], bank[:, u * 4 + q]).then_inc(taken_v, 1)

                prepare(0, 0, True)
                body(0, True, False)
                with dve.Fori(1, E4 // 2 - 1) as j:
                    body(j, False, False)
                body(E4 // 2 - 1, False, True)

            @block.tensor
            def _(pe):
                def body(j, first):
                    for u in range(2):
                        e = j * 2 + u
                        pe.wait_ge(w_lo_done, e + 1)
                        pe.wait_ge(d_hi_done, e + 1)
                        pe.wait_ge(d_lo_done, e + 1)
                        for q in range(4):
                            if not first:
                                if q < 2:
                                    pe.wait_ge(taken_a, (e - 2) * 2 + q + 1)
                                else:
                                    pe.wait_ge(taken_v, (e - 2) * 2 + q - 1)
                            out = bank[:, u * 4 + q]
                            pe.matmul(out, d_hi[:, u, q], w_hi[:, u], start=True, stop=False)
                            pe.matmul(out, d_hi[:, u, q], w_lo[:, u], start=False, stop=False)
                            pe.matmul(out, d_lo[:, u, q], w_hi[:, u], start=False, stop=True).then_inc(made, 1)

                body(0, True)
                with pe.Fori(1, E4 // 2) as j:
                    body(j, False)


def combine(nc, a, m, inner):
    NTL = T // P
    GQ = P // GT
    with ExitStack() as ctx:
        def sb(name, shape, dt):
            return ctx.enter_context(nc.sbuf_tensor(name, shape, dt))

        def sem(name):
            return ctx.enter_context(nc.semaphore(name))

        U = 4
        y = sb("y_in", [P, U, GQ, D], F32)
        pick = sb("pick_in", [P, U, P], F32)
        x2 = sb("x2_in", [P, U, D], F32)
        out = sb("out_sb", [P, U, D], F32)
        bank = ctx.enter_context(nc.psum_tensor("p5_bank", [P, 8, 512], F32))
        loaded = [sem(f"y_loaded{i}") for i in range(U)]
        stored = [sem(f"out_stored{i}") for i in range(U)]
        summed = sem("summed")
        added = sem("added")

        x2_src = m.x2.rearrange("(i p) d -> i p d", p=P)
        y_src = m.y.rearrange("(i g) e d -> i e g d", g=GQ)
        o_dst = a.out.rearrange("b (n p) d -> (b n) p d", p=P)

        with nc.Block() as block:
            @block.sync
            def _(sp):
                def load(i, u):
                    sp.dma_start(y[:, u], y_src[i]).then_inc(loaded[u], 16)
                    sp.dma_start(pick[:, u], m.pick[i]).then_inc(loaded[u], 16)
                    sp.dma_start(x2[:, u], x2_src[i]).then_inc(loaded[u], 16)

                for u in range(U):
                    load(u, u)
                with sp.Fori(0, NTL // U - 1) as j:
                    for u in range(U):
                        ahead, done = held(sp, j * U + U + u), held(sp, j * U + u + 1)
                        sp.wait_ge(added, done)
                        load(ahead, u)

            @block.scalar
            def _(act):
                def body(j):
                    for u in range(U):
                        act.wait_ge(added, j * U + u + 1)
                        act.dma_start(o_dst[j * U + u], out[:, u]).then_inc(stored[u], 16)

                with act.Fori(0, NTL // U) as j:
                    body(j)
                for u in range(U):
                    act.wait_ge(stored[u], 16 * NTL // U)

            @block.vector
            def _(dve):
                def body(j, first):
                    for u in range(U):
                        dve.wait_ge(summed, j * U + u + 1)
                        if not first:
                            dve.wait_ge(stored[u], j * 16)
                        dve.tensor_tensor(out[:, u], bank[:, u], x2[:, u], ALU.add).then_inc(added, 1)

                body(0, True)
                with dve.Fori(1, NTL // U) as j:
                    body(j, False)

            @block.tensor
            def _(pe):
                def body(j, first):
                    for u in range(U):
                        pe.wait_ge(loaded[u], j * 48 + 48)
                        if not first:
                            pe.wait_ge(added, j * U + u - (U - 1))
                        for g in range(GQ):
                            mm = pe.matmul(bank[g * GT:(g + 1) * GT, u], pick[:, u, g * GT:(g + 1) * GT], y[:, u, g],
                                           start=True, stop=True, tile_position=(0, g * GT))
                        mm.then_inc(summed, 1)

                body(0, True)
                with pe.Fori(1, NTL // U) as j:
                    body(j, False)


def build(nc, a, m, phases=(1, 2, 3, 4, 5)):
    if 1 in phases:
        project(nc, a, m)
    if 2 in phases:
        attend(nc, a, m)
    with nc.sbuf_tensor("inner", [P, E4, NGR], F32) as inner:
        for n, phase in ((3, dispatch), (4, expand), (5, combine)):
            if n in phases:
                phase(nc, a, m, inner)


def layout(**inputs):
    import numpy as np

    def arr(x):
        return np.ascontiguousarray(np.asarray(x))

    i = inputs
    ctx = arr(i["ctx_1024"])
    r = np.arange(P)
    ban = np.where(r[:, None] >= r[None, :], np.float32(MASKED), np.float32(0))
    ban0 = ban.copy()
    ban0[0, 0] = 0.0
    out = {
        "x": arr(i["x"]),
        "ctx_t": arr(ctx.reshape(NCH, CH, D).transpose(0, 2, 1)),
        "wq_t": arr(arr(i["L0_xattn_Wq"]).T),
        "wk_t": arr(arr(i["L0_xattn_Wk"]).T),
        "wv_t": arr(arr(i["L0_xattn_Wv"]).T),
        "wo_t": arr(arr(i["L0_xattn_Wo"]).T),
        "bv": arr(i["L0_xattn_bv"]),
        "bo": arr(i["L0_xattn_bo"]),
        "controller": arr(i["L0_ffn_controller"]).reshape(D, NE),
        "f1": arr(i["L0_ffn_f1"]).reshape(D, NE * F),
        "bias_col": arr(arr(i["L0_ffn_bias"]).reshape(E4, P).T),
        "f2": arr(i["L0_ffn_f2"]).reshape(NE * F, D),
        "ident": np.eye(P, dtype=np.float32),
        "mask_ts": np.stack([ban, ban0]),
        "mask_st": arr(np.stack([ban.T, ban0.T])),
        "tie_row": np.linspace(0.0, 1e-6, GT, dtype=np.float32),
        "block_cols": arr((r[:, None] // 32 == np.arange(4)[None, :]).astype(np.float32)),
    }
    return out


def kernel(**inputs):
    import numpy as np
    import concourse.bacc as bacc
    from concourse.bass_utils import run_bass_kernel_spmd

    nc = bacc.Bacc("TRN2", target_bir_lowering=False, num_devices=1)
    arrays, a = {}, Plan()
    for name, x in layout(**inputs).items():
        arrays["in_" + name] = x
        a.__dict__[name] = nc.dram_tensor("in_" + name, x.shape, mybir.dt.from_np(x.dtype), kind="ExternalInput").ap()
    a.out = nc.dram_tensor("out", (B, S, D), F32, kind="ExternalOutput").ap()
    build(nc, a, scratch(nc))
    r = run_bass_kernel_spmd(nc, [arrays], core_ids=[0])
    return r.results[0]["out"]
```

```python
from contextlib import ExitStack

import concourse.bass as bass
from concourse import mybir

F32 = mybir.dt.float32
F32R = mybir.dt.float32r
BF16 = mybir.dt.bfloat16
ALU = mybir.AluOpType
ACT = mybir.ActivationFunctionType
AX = mybir.AxisListType

P = 128
B, S, D = 4, 1024, 512
H, HD = 16, 32
HG = 4
NG = H // HG
T = B * S
CH = 512
NCH = T // CH
KD = D // P
TT = CH // P
E, ES = 32, 4
NE = E * ES
F = 32
GT = E
NGR = T // GT
E4 = NE // 4
EPS = 1e-5
SCALE = float(HD) ** -0.5
MASKED = -1e30


class Plan:
    pass


def scratch(nc):
    m = Plan()
    m.q_hi = nc.dram_tensor("q_hi", (NG, P, T), F32).ap()
    m.q_lo = nc.dram_tensor("q_lo", (NG, P, T), F32).ap()
    m.k_hi = nc.dram_tensor("k_hi", (NG, P, T), F32).ap()
    m.k_lo = nc.dram_tensor("k_lo", (NG, P, T), F32).ap()
    m.v = nc.dram_tensor("v_rows", (T, D), F32).ap()
    m.o = nc.dram_tensor("o_t", (NG, P, T), F32).ap()
    m.pick = nc.dram_tensor("pick_rows", (T // P, NE, P), F32).ap()
    m.x2 = nc.dram_tensor("x_mid", (T, D), F32).ap()
    return m


def held(eng, value):
    return value if isinstance(value, int) else eng.snap(value)


def project(nc, a, m):
    with ExitStack() as ctx:
        def sb(name, shape, dt):
            return ctx.enter_context(nc.sbuf_tensor(name, shape, dt))

        def sem(name):
            return ctx.enter_context(nc.semaphore(name))

        w_raw = sb("w_raw", [P, 3, KD, D], F32)
        w_hi = sb("w_hi", [P, 3, KD, D], F32R)
        w_lo = sb("w_lo", [P, 3, KD, D], F32R)
        bv_row = sb("bv_row", [P, D], F32)
        ident = sb("ident", [P, P], F32)
        x_in = sb("x_in", [P, TT, D], F32)
        xn = sb("xn", [P, TT, D], F32)
        c_in = sb("c_in", [P, KD, CH], F32)
        c_hi = sb("c_hi", [P, KD, CH], F32R)
        c_lo = sb("c_lo", [P, KD, CH], F32R)
        t_hi = sb("t_hi", [P, KD, CH], F32R)
        t_lo = sb("t_lo", [P, KD, CH], F32R)
        k_hi = sb("k_hi_s", [P, NG, CH], F32R)
        k_lo = sb("k_lo_s", [P, NG, CH], F32R)
        q_hi = sb("q_hi_s", [P, NG, CH], F32R)
        q_lo = sb("q_lo_s", [P, NG, CH], F32R)
        v_out = sb("v_out", [P, TT, D], F32)
        stats = sb("stats", [P, TT, 6], F32)
        mv = sb("mv", [P, TT, 2], F32)
        ve = sb("ve", [P, TT], F32)
        sd = sb("sd", [P, TT], F32)
        r0 = sb("r0", [P, TT], F32)
        r1 = sb("r1", [P, TT], F32)
        r2 = sb("r2", [P, TT], F32)
        rstd = sb("rstd", [P, TT], F32)
        gate = sb("gate", [P, 1], F32)
        bank = ctx.enter_context(nc.psum_tensor("p1_bank", [P, 8, 512], F32))

        W_ORDER = (1, 2, 0)
        consts_in = sem("consts_in")
        w_in = [sem(f"w_in{i}") for i in range(3)]
        w_hi_done = sem("w_hi_done")
        w_lo_done = sem("w_lo_done")
        x_loaded = sem("x_loaded")
        c_loaded = sem("c_loaded")
        c_hi_done = sem("c_hi_done")
        c_lo_done = sem("c_lo_done")
        chain = sem("chain")
        sd_ready = sem("sd_ready")
        xn_ready = sem("xn_ready")
        filled = sem("filled")
        hi_done = sem("hi_done")
        lo_done = sem("lo_done")
        k_stored = sem("k_stored")
        q_stored = sem("q_stored")
        v_stored = sem("v_stored")

        xr = a.x.rearrange("b s d -> (b s) d").rearrange("(c t p) d -> c p t d", t=TT, p=P)
        cr = a.ctx_t.rearrange("c (k p) s -> c p k s", p=P)
        vr = m.v.rearrange("(c t p) d -> c p t d", t=TT, p=P)

        by_chunk = {n: x.rearrange("g p (c s) -> c p g s", c=NCH) for n, x in
                    (("k_hi", m.k_hi), ("k_lo", m.k_lo), ("q_hi", m.q_hi), ("q_lo", m.q_lo))}

        GPC = 16
        APC = 12
        CHAIN = 8

        with nc.Block() as block:
            @block.sync
            def _(sp):
                sp.dma_start(x_in[:], xr[0]).then_inc(x_loaded, 16)
                sp.dma_start(ident[:], a.ident).then_inc(consts_in, 16)
                sp.dma_start(bv_row[:], a.bv.unsqueeze(0).broadcast_to([P, D])).then_inc(consts_in, 16)
                sp.dma_start(c_in[:], cr[0]).then_inc(c_loaded, 16)
                for i in W_ORDER:
                    w = (a.wq_t, a.wk_t, a.wv_t)[i]
                    sp.dma_start(w_raw[:, i], w.rearrange("(k p) n -> p k n", p=P)).then_inc(w_in[i], 16)

                def body(c, last):
                    cur, nxt = held(sp, c), held(sp, c + 1)
                    x_free, k_done = held(sp, c * TT + TT), held(sp, c * GPC + 8)
                    v_done, q_done = held(sp, c * GPC + 12), held(sp, c * GPC + 16)
                    if not last:
                        sp.wait_ge(xn_ready, x_free)
                        sp.dma_start(x_in[:], xr[nxt]).then_inc(x_loaded, 16)
                        sp.wait_ge(c_lo_done, nxt)
                        sp.dma_start(c_in[:], cr[nxt]).then_inc(c_loaded, 16)
                    sp.wait_ge(lo_done, k_done)
                    sp.dma_start(by_chunk["k_hi"][cur], k_hi[:].bitcast(F32)).then_inc(k_stored, 16)
                    sp.dma_start(by_chunk["k_lo"][cur], k_lo[:].bitcast(F32)).then_inc(k_stored, 16)
                    sp.wait_ge(lo_done, v_done)
                    sp.dma_start(vr[cur], v_out[:]).then_inc(v_stored, 16)
                    sp.wait_ge(lo_done, q_done)
                    sp.dma_start(by_chunk["q_hi"][cur], q_hi[:].bitcast(F32)).then_inc(q_stored, 16)
                    sp.dma_start(by_chunk["q_lo"][cur], q_lo[:].bitcast(F32)).then_inc(q_stored, 16)

                with sp.Fori(0, NCH - 1) as c:
                    body(c, False)
                body(NCH - 1, True)
                sp.wait_ge(k_stored, 32 * NCH)
                sp.wait_ge(v_stored, 16 * NCH)
                sp.wait_ge(q_stored, 32 * NCH)

            @block.scalar
            def _(act):
                def weight_hi(n):
                    i = W_ORDER[n]
                    act.wait_ge(w_in[i], 16)
                    act.copy(w_hi[:, i], w_raw[:, i]).then_inc(w_hi_done, 1)

                def next_chunk_sd(c):
                    act.wait_ge(chain, c * CHAIN + 3)
                    act.activation(sd[:], ve[:], ACT.Sqrt).then_inc(sd_ready, 1)

                def next_chunk_hi(c, first):
                    act.wait_ge(c_loaded, 16 * c + 16)
                    if not first:
                        act.wait_ge(filled, (c - 1) * GPC + 12)
                    act.copy(c_hi[:], c_in[:]).then_inc(c_hi_done, 1)

                next_chunk_sd(0)
                next_chunk_hi(0, True)
                weight_hi(0)

                def body(c, first, last):
                    for k in range(KD):
                        act.wait_ge(filled, c * GPC + k + 1)
                        act.copy(t_hi[:, k], bank[:, k]).then_inc(hi_done, 1)
                    if first:
                        weight_hi(1)
                        weight_hi(2)
                    for g in range(NG):
                        act.wait_ge(filled, c * GPC + 4 + g + 1)
                        if not first and g == 0:
                            act.wait_ge(k_stored, 32 * c)
                        act.copy(k_hi[:, g], bank[:, 4 + g]).then_inc(hi_done, 1)
                    if not last:
                        next_chunk_sd(c + 1)
                        next_chunk_hi(c + 1, False)
                    for g in range(NG):
                        act.wait_ge(filled, c * GPC + 12 + g + 1)
                        if not first and g == 0:
                            act.wait_ge(q_stored, 32 * c)
                        act.copy(q_hi[:, g], bank[:, 4 + g]).then_inc(hi_done, 1)

                body(0, True, False)
                with act.Fori(1, NCH - 1) as c:
                    body(c, False, False)
                body(NCH - 1, False, True)

            @block.vector
            def _(dve):
                def link(c, n, ins):
                    ins.then_inc(chain, 1)
                    dve.wait_ge(chain, c * CHAIN + n)

                def ln_rstd(c, n):
                    dve.wait_ge(sd_ready, c + 1)
                    link(c, n, dve.reciprocal(r0[:], sd[:]))
                    link(c, n + 1, dve.tensor_tensor(r1[:], r0[:], r0[:], ALU.mult))
                    link(c, n + 2, dve.tensor_tensor(r2[:], r1[:], ve[:], ALU.mult))
                    link(c, n + 3, dve.tensor_scalar(r1[:], r2[:], -0.5, 1.5, ALU.mult, ALU.add))
                    link(c, n + 4, dve.tensor_tensor(rstd[:], r0[:], r1[:], ALU.mult))

                def ln_apply(c, t, first):
                    if not first and t == 0:
                        dve.wait_ge(filled, (c - 1) * GPC + 4)
                    dve.tensor_scalar(xn[:, t], x_in[:, t], mv[:, t, 0:1], rstd[:, t:t + 1],
                                      ALU.subtract, ALU.mult).then_inc(xn_ready, 1)

                def ctx_lo(c, first):
                    dve.wait_ge(c_hi_done, c + 1)
                    dve.tensor_tensor(c_lo[:], c_in[:], c_hi[:].bitcast(F32), ALU.subtract).then_inc(c_lo_done, 1)

                def stats_all(c):
                    dve.wait_ge(x_loaded, 16 * c + 16)
                    for t in range(TT):
                        ins = dve.bn_stats(stats[:, t], x_in[:, t])
                    link(c, 1, ins)
                    dve.memset(gate[:], 0.0)
                    for t in range(TT):
                        ins = dve.bn_aggr(mv[:, t], stats[:, t])
                    link(c, 2, ins)
                    link(c, 3, dve.tensor_scalar(ve[:], mv[:, :, 1], EPS, None, ALU.add))

                stats_all(0)
                ln_rstd(0, 4)
                for t in range(TT):
                    ln_apply(0, t, True)
                ctx_lo(0, True)

                def weight_lo(n):
                    i = W_ORDER[n]
                    dve.wait_ge(w_hi_done, n + 1)
                    dve.tensor_tensor(w_lo[:, i], w_raw[:, i], w_hi[:, i].bitcast(F32),
                                      ALU.subtract).then_inc(w_lo_done, 1)

                weight_lo(0)

                def body(c, first, last):
                    for k in range(KD):
                        dve.wait_ge(hi_done, c * APC + k + 1)
                        dve.tensor_tensor(t_lo[:, k], bank[:, k], t_hi[:, k].bitcast(F32),
                                          ALU.subtract).then_inc(lo_done, 1)
                    if first:
                        dve.wait_ge(consts_in, 32)
                        weight_lo(1)
                        weight_lo(2)
                    for g in range(NG):
                        dve.wait_ge(hi_done, c * APC + 4 + g + 1)
                        dve.tensor_tensor(k_lo[:, g], bank[:, 4 + g], k_hi[:, g].bitcast(F32),
                                          ALU.subtract).then_inc(lo_done, 1)
                    if not last:
                        stats_all(c + 1)
                    for t in range(TT):
                        dve.wait_ge(filled, c * GPC + 8 + t + 1)
                        if not first and t == 0:
                            dve.wait_ge(v_stored, 16 * c)
                        dve.tensor_tensor(v_out[:, t], bank[:, t], bv_row[:], ALU.add).then_inc(lo_done, 1)
                        if not last and t == 0:
                            ln_rstd(c + 1, 4)
                        if not last:
                            ln_apply(c + 1, t, False)
                    if not last:
                        ctx_lo(c + 1, False)
                    for g in range(NG):
                        dve.wait_ge(hi_done, c * APC + 8 + g + 1)
                        dve.tensor_tensor(q_lo[:, g], bank[:, 4 + g], q_hi[:, g].bitcast(F32),
                                          ALU.subtract).then_inc(lo_done, 1)

                body(0, True, False)
                with dve.Fori(1, NCH - 1) as c:
                    body(c, False, False)
                body(NCH - 1, False, True)

            @block.tensor
            def _(pe):
                pe.wait_ge(consts_in, 32)

                def split_product(out, lhs, rhs):
                    for k in range(KD):
                        (lh, ll), (rh, rl) = lhs(k), rhs(k)
                        pe.matmul(out, lh, rh, start=(k == 0), stop=False)
                        pe.matmul(out, lh, rl, start=False, stop=False)
                        mm = pe.matmul(out, ll, rh, start=False, stop=(k == KD - 1))
                    mm.then_inc(filled, 1)

                def body(c, first):
                    pe.wait_ge(xn_ready, c * TT + TT)
                    for k in range(KD):
                        if not first:
                            pe.wait_ge(lo_done, (c - 1) * GPC + 8 + k + 1)
                        for t in range(TT):
                            mm = pe.transpose(bank[:, k, t * P:(t + 1) * P], xn[:, t, k * P:(k + 1) * P], ident[:])
                        mm.then_inc(filled, 1)
                    pe.wait_ge(c_lo_done, c + 1)
                    if first:
                        pe.wait_ge(w_lo_done, 1)
                    for g in range(NG):
                        if not first:
                            pe.wait_ge(lo_done, (c - 1) * GPC + 12 + g + 1)
                        split_product(bank[:, 4 + g],
                                      lambda k: [w[:, 1, k, g * P:(g + 1) * P] for w in (w_hi, w_lo)],
                                      lambda k: [c_hi[:, k], c_lo[:, k]])
                    if first:
                        pe.wait_ge(w_lo_done, 2)
                    for t in range(TT):
                        pe.wait_ge(lo_done, c * GPC + t + 1)
                        split_product(bank[:, t],
                                      lambda k: [x[:, k, t * P:(t + 1) * P] for x in (c_hi, c_lo)],
                                      lambda k: [w_hi[:, 2, k], w_lo[:, 2, k]])
                    if first:
                        pe.wait_ge(w_lo_done, 3)
                    for g in range(NG):
                        pe.wait_ge(lo_done, c * GPC + 4 + g + 1)
                        split_product(bank[:, 4 + g],
                                      lambda k: [w[:, 0, k, g * P:(g + 1) * P] for w in (w_hi, w_lo)],
                                      lambda k: [t_hi[:, k], t_lo[:, k]])

                body(0, True)
                with pe.Fori(1, NCH) as c:
                    body(c, False)


def attend(nc, a, m):
    NIT = B * NG
    ST = S // P
    SLOTS = 3
    R = 3 * HD
    STEPS = [(0, 0), (0, 3), (0, 1), (0, 2)] + [(1, j) for j in (4, 0, 5, 1, 6, 2, 7, 3)]
    NS = len(STEPS)
    WIDTH = [CH * (sh + 1) - max(CH * sh, P * j) for sh, j in STEPS]
    DIAG = [k for k, (sh, j) in enumerate(STEPS) if P * j >= CH * sh]
    CHUNKS = []
    for h in range(HG):
        for i in range(ST):
            if i >= 4:
                CHUNKS.append((h, i, 0, CH, False))
            t0 = CH * (i // 4)
            CHUNKS.append((h, i, t0, (i + 1) * P - t0, True))
    NC = len(CHUNKS)
    MAX_STEPS = 9
    LOADS = 7 * 16
    DUE = [NC * sum(WIDTH[:k]) // sum(WIDTH[:MAX_STEPS]) for k in range(MAX_STEPS + 1)]
    RP = 8
    RW = CH // RP
    AFTER = {6 + 3 * q: q for q in range(RP)}

    with ExitStack() as ctx:
        def sb(name, shape, dt):
            return ctx.enter_context(nc.sbuf_tensor(name, shape, dt))

        def sem(name):
            return ctx.enter_context(nc.semaphore(name))

        ks = [sb(f"k_stack{i}", [P, HG, S], F32R) for i in range(SLOTS)]
        qs = [sb(f"q_stack{i}", [P, HG, S], F32R) for i in range(SLOTS)]
        vt = [sb(f"v_tile{i}", [P, ST, P], F32) for i in range(SLOTS)]
        pt = sb("p_t", [P, 2, HG, CH], F32)
        mask_f = sb("mask_f", [P, 2, P], F32)
        mask_st = sb("mask_st", [P, 2, P], BF16)
        ident = sb("ident2", [P, P], F32)
        ident_b = sb("ident_b", [P, P], BF16)
        ones = sb("ones", [P, HD], F32)
        mx_a = sb("mx_a", [P, HG * ST], F32)
        mx_b = sb("mx_b", [P, HG * ST], F32)
        mx = sb("mx", [P, HG * ST], F32)
        m_row = sb("m_row", [HG * ST, P], F32R)
        o_sb = sb("o_sb", [P, 2, CH], F32)
        d_sb = sb("d_sb", [P, 2, CH], F32)
        r_sb = sb("r_sb", [P, 2, CH], F32)
        o_n = sb("o_n", [P, 2, CH], F32)
        bank = ctx.enter_context(nc.psum_tensor("p2_bank", [P, 8, 512], F32))
        MX, OB, DB = 4, 6, 7

        const_in = sem("const_in")
        const_ready = sem("const_ready")
        row_ready = sem("row_ready")
        loaded = [sem(f"loaded{i}") for i in range(SLOTS)]
        scored = sem("scored")
        exp_done = sem("exp_done")
        masked = sem("masked")
        step_done = sem("step_done")
        mx_filled = sem("mx_filled")
        mx_read = sem("mx_read")
        mx_ready = sem("mx_ready")
        mx_turned = sem("mx_turned")
        m_row_ready = sem("m_row_ready")
        m_placed = sem("m_placed")
        o_read = sem("o_read")
        inverted = sem("inverted")
        divided = sem("divided")
        o_stored = [sem(f"o_stored{i}") for i in range(2)]

        def load(eng, it, slot):
            b, g = it // NG, it % NG
            for stack, parts in ((ks[slot], (m.k_hi, m.k_lo, m.k_hi)), (qs[slot], (m.q_hi, m.q_hi, m.q_lo))):
                for r, part in enumerate(parts):
                    src = part.rearrange("g (h p) (b s) -> b g p h s", p=HD, b=B)[b, g]
                    eng.dma_start(stack[r * HD:(r + 1) * HD].bitcast(F32), src).then_inc(loaded[slot], 16)
            src = m.v.rearrange("(b t p) (g n) -> b g p t n", b=B, p=P, g=NG)[b, g]
            eng.dma_start(vt[slot][:], src).then_inc(loaded[slot], 16)

        with nc.Block() as block:
            @block.sync
            def _(sp):
                sp.dma_start(mask_f[:], a.mask_st.rearrange("v s t -> s v t")).then_inc(const_in, 16)
                sp.dma_start(ident[:], a.ident).then_inc(const_in, 16)
                load(sp, 0, 0)
                load(sp, 1, 1)

                def place_max(it, slot):
                    sp.wait_ge(m_row_ready, it)
                    sp.dma_start(qs[slot][R:R + 1].rearrange("p h s -> p (h s)").bitcast(F32),
                                 m_row[:].bitcast(F32)).then_inc(m_placed, 16)

                def store(it, half, n):
                    sp.wait_ge(divided, n)
                    sp.dma_start(m.o.rearrange("g p (b s) -> b g p s", b=B)[it // NG, it % NG][:, half * CH:(half + 1) * CH],
                                 o_n[:, half]).then_inc(o_stored[half], 16)

                def body(it, slot, first, last, more):
                    prev = held(sp, it - 1)
                    ahead = held(sp, it + 2)
                    steps, two_it = held(sp, it * NS), held(sp, it * 2)
                    this_half, place_at = held(sp, it * 2 - 1), held(sp, it + 2)
                    if more:
                        if not first:
                            sp.wait_ge(step_done, steps)
                        load(sp, ahead, (slot + 2) % SLOTS)
                    if not first:
                        store(prev, 0, this_half)
                        store(prev, 1, two_it)
                    if not last:
                        place_max(place_at, (slot + 1) % SLOTS)

                place_max(1, 0)
                body(0, 0, True, False, True)
                with sp.Fori(0, (NIT - 4) // SLOTS) as g:
                    for u in range(SLOTS):
                        body(g * SLOTS + (1 + u), (1 + u) % SLOTS, False, False, True)
                for it in range(NIT - 3, NIT):
                    body(it, it % SLOTS, False, it == NIT - 1, it + 2 < NIT)
                store(NIT - 1, 0, 2 * NIT - 1)
                store(NIT - 1, 1, 2 * NIT)
                for half in range(2):
                    sp.wait_ge(o_stored[half], 16 * NIT)

            @block.gpsimd
            def _(pool):
                pool.wait_ge(const_in, 32)
                pool.tensor_copy(ident_b[:], ident[:]).then_inc(const_ready, 1)
                pool.tensor_copy(mask_st[:], mask_f[:]).then_inc(const_ready, 1)
                pool.wait_ge(const_ready, 4)
                for i in range(SLOTS):
                    pool.memset(ks[i][R:R + 1].bitcast(F32), 1.0).then_inc(row_ready, 1)

                def mask(it, k):
                    first_tile = STEPS[k][1] == 0
                    e0 = ident[:, 0:1]
                    for h in range(HG):
                        pool.wait_ge(exp_done, (it * NS + k) * HG + h + 1)
                        pool.tensor_tensor(pt[:, k % 2, h, 0:1], e0, e0, ALU.mult if first_tile else ALU.subtract)
                        part = pt[:, k % 2, h, 1:P]
                        pool.affine_select(part, part, [[1, P - 1]], ALU.is_ge, 0.0, base=0,
                                           channel_multiplier=-1).then_inc(masked, 1)

                def divide(it, half, first):
                    pool.wait_ge(inverted, (it * 2 + half) * RP + RP)
                    if not first:
                        pool.wait_ge(o_stored[half], it * 16)
                    pool.tensor_tensor(o_n[:, half], o_sb[:, half], r_sb[:, half], ALU.mult).then_inc(divided, 1)

                def body(it, first, second):
                    for k in DIAG:
                        mask(it, k)
                        if k == 0 and not first:
                            divide(it - 1, 0, second)
                        if k == 8 and not first:
                            divide(it - 1, 1, second)

                body(0, True, False)
                body(1, False, True)
                with pool.Fori(2, NIT) as it:
                    body(it, False, False)
                divide(NIT - 1, 0, False)
                divide(NIT - 1, 1, False)

            @block.vector
            def _(dve):
                dve.memset(ones[:], 1.0).then_inc(const_ready, 1)
                dve.memset(mx_b[:], -3e38).then_inc(const_ready, 1)
                dve.wait_ge(const_ready, 4)

                def invert(hf, half, q, first):
                    if q == 0:
                        dve.wait_ge(o_read, hf * 2 + 2)
                        if not first:
                            dve.wait_ge(divided, hf - 1)
                    dve.reciprocal(r_sb[:, half, q * RW:(q + 1) * RW], d_sb[:, half, q * RW:(q + 1) * RW]
                                   ).then_inc(inverted, 1)

                def maxima(it, first, older, older_first):
                    for n, (h, i, t0, w, diag) in enumerate(CHUNKS):
                        if n == 0 and not first:
                            dve.wait_ge(mx_ready, it)
                        dve.wait_ge(mx_filled, it * NC + n + 1)
                        to = mx_a if t0 == 0 else mx_b
                        dve.tensor_reduce(to[:, h * ST + i:h * ST + i + 1], bank[:, MX + n % (4 if first else 2), 0:w], AX.X,
                                          ALU.max).then_inc(mx_read, 1)
                        if n in AFTER and older:
                            invert(it * 2 - 3, 1, AFTER[n], older_first)
                    dve.wait_ge(mx_read, it * NC + NC)
                    if not first:
                        dve.wait_ge(mx_turned, it)
                    dve.tensor_tensor(mx[:], mx_a[:], mx_b[:], ALU.max).then_inc(mx_ready, 1)
                    if not first:
                        for q in range(RP):
                            invert(it * 2 - 2, 0, q, not older)

                maxima(0, True, False, False)
                maxima(1, False, False, False)
                maxima(2, False, True, True)
                with dve.Fori(3, NIT) as it:
                    maxima(it, False, True, False)
                for hf in range(2 * NIT - 3, 2 * NIT):
                    for q in range(RP):
                        invert(hf, hf % 2, q, False)

            @block.scalar
            def _(act):
                def negate(it, first):
                    act.wait_ge(mx_turned, it + 1)
                    if not first:
                        act.wait_ge(m_placed, it * 16)
                    act.activation(m_row[:], bank[0:HG * ST, MX, 0:P], ACT.Copy, scale=-1.0).then_inc(m_row_ready, 1)

                def take(it, half, first):
                    act.wait_ge(step_done, it * NS + (4 if half == 0 else NS))
                    if not first:
                        act.wait_ge(divided, it * 2 + half - 1)
                    act.copy(o_sb[:, half], bank[:, OB]).then_inc(o_read, 1)
                    act.copy(d_sb[:, half], bank[:, DB]).then_inc(o_read, 1)

                def body(it, first, last):
                    for k, (sh, j) in enumerate(STEPS):
                        w = CH * (sh + 1) - max(CH * sh, P * j)
                        for h in range(HG):
                            act.wait_ge(scored, (it * NS + k) * HG + h + 1)
                            if h == 0 and not (first and k < 2):
                                act.wait_ge(step_done, it * NS + k - 1)
                            act.activation(pt[:, k % 2, h, 0:w], bank[:, h, 0:w], ACT.Exp,
                                           scale=SCALE).then_inc(exp_done, 1)
                        if k == 0 and not first:
                            take(it - 1, 1, False) if not isinstance(it, int) or it > 1 else take(0, 1, True)
                        if k == 4:
                            take(it, 0, first)
                        if k == MAX_STEPS and not last:
                            negate(it + 1, False)

                negate(0, True)
                body(0, True, False)
                body(1, False, False)
                with act.Fori(2, NIT - 1) as it:
                    body(it, False, False)
                body(NIT - 1, False, True)
                take(NIT - 1, 1, False)

            @block.tensor
            def _(pe):
                pe.wait_ge(const_ready, 4)

                def chunk(it, n, slot, first):
                    h, i, t0, w, diag = CHUNKS[n]
                    if n == 0 and not first:
                        pe.wait_ge(m_row_ready, it)
                    ring = 4 if first else 2
                    if not (first and n < ring):
                        pe.wait_ge(mx_read, it * NC + n - ring + 1)
                    to = MX + n % ring
                    out = bank[:, to, 0:w]
                    mm = pe.matmul(out, qs[slot][0:R, h, i * P:(i + 1) * P], ks[slot][0:R, h, t0:t0 + w],
                                   start=True, stop=not diag)
                    if diag:
                        mm = pe.matmul(bank[:, to, w - P:w], ident_b[:], mask_st[:, 1 if i == 0 else 0],
                                       start=False, stop=True)
                    mm.then_inc(mx_filled, 1)

                def turn(it):
                    pe.wait_ge(mx_ready, it + 1)
                    pe.transpose(bank[0:HG * ST, MX, 0:P], mx[:], ident[:]).then_inc(mx_turned, 1)

                def scores(it, k, slot, first, heads):
                    sh, j = STEPS[k]
                    s0 = max(CH * sh, P * j)
                    w = CH * (sh + 1) - s0
                    if k == 0 and heads[0] == 0:
                        pe.wait_ge(m_placed, it * 16 + 16)
                    for h in heads:
                        if not (first and k == 0):
                            pe.wait_ge(exp_done, (it * NS + k - 1) * HG + h + 1)
                        pe.matmul(bank[:, h, 0:w], ks[slot][0:R + 1, h, j * P:(j + 1) * P],
                                  qs[slot][0:R + 1, h, s0:s0 + w], start=True, stop=True).then_inc(scored, 1)

                def values(it, k, slot, first):
                    sh, j = STEPS[k]
                    s0 = max(CH * sh, P * j)
                    w = CH * (sh + 1) - s0
                    c0 = s0 - CH * sh
                    if k in (0, 4) and not (first and k == 0):
                        pe.wait_ge(o_read, (it * 2 + sh) * 2)
                    for h in range(HG):
                        if k in DIAG:
                            pe.wait_ge(masked, (it * len(DIAG) + DIAG.index(k)) * HG + h + 1)
                        else:
                            pe.wait_ge(exp_done, (it * NS + k) * HG + h + 1)
                        pe.matmul(bank[h * HD:(h + 1) * HD, OB, c0:c0 + w], vt[slot][:, j, h * HD:(h + 1) * HD],
                                  pt[:, k % 2, h, 0:w], start=(k in (0, 4)), stop=(k in (3, NS - 1)),
                                  tile_position=(0, h * HD), skip_group_check=True)

                def sums(k):
                    sh, j = STEPS[k]
                    c0 = max(0, P * j - CH * sh)
                    w = CH - c0
                    for h in range(HG):
                        mm = pe.matmul(bank[h * HD:(h + 1) * HD, DB, c0:c0 + w], ones[:],
                                       pt[:, k % 2, h, 0:w], start=(k in (0, 4)), stop=(k in (3, NS - 1)),
                                       tile_position=(0, h * HD), skip_group_check=True)
                    mm.then_inc(step_done, 1)

                def body(it, slot, first, last, load_count):
                    nslot = (slot + 1) % SLOTS
                    for k in range(NS):
                        due = []
                        if not last:
                            if k == 0:
                                pe.wait_ge(loaded[nslot], load_count)
                            if k < MAX_STEPS:
                                due = list(range(DUE[k], DUE[k + 1]))

                        def some(parts_left):
                            for _ in range(-(-len(due) // parts_left)):
                                chunk(it + 1, due.pop(0), nslot, False)

                        nxt = (it, k + 1, slot) if k < NS - 1 else None if last else (it + 1, 0, nslot)
                        if nxt:
                            scores(*nxt, False, (0, 1))
                        some(4)
                        if nxt:
                            scores(*nxt, False, (2, 3))
                        if k == MAX_STEPS and not last:
                            turn(it + 1)
                        some(3)
                        values(it, k, slot, first)
                        some(2)
                        sums(k)
                        some(1)

                pe.wait_ge(loaded[0], LOADS)
                for n in range(NC):
                    chunk(0, n, 0, True)
                turn(0)
                pe.wait_ge(row_ready, SLOTS)
                scores(0, 0, 0, True, range(HG))
                body(0, 0, True, False, LOADS)
                with pe.Fori(0, (NIT - 4) // SLOTS) as g:
                    for u in range(SLOTS):
                        body(g * SLOTS + (1 + u), (1 + u) % SLOTS, False, False,
                             (g + (2 + u) // SLOTS + 1) * LOADS)
                for it in range(NIT - 3, NIT):
                    body(it, it % SLOTS, False, it == NIT - 1, ((it + 1) // SLOTS + 1) * LOADS)


def dispatch(nc, a, m, inner):
    NT = S // P
    GB = S // GT
    GQ = P // GT
    CHAIN = 7

    with ExitStack() as ctx:
        def sb(name, shape, dt):
            return ctx.enter_context(nc.sbuf_tensor(name, shape, dt))

        def sem(name):
            return ctx.enter_context(nc.semaphore(name))

        f1 = sb("f1_sb", [P, KD, NE * F], F32)
        disp = sb("disp_t", [P, KD, NE, GB], F32)
        wo_raw = disp[:, 0, 0:NE // 2].rearrange("p e g -> p (e g)").rearrange("p (k n) -> p k n", k=KD)
        wo_hi = sb("wo_hi", [P, KD, D], F32R)
        wo_lo = sb("wo_lo", [P, KD, D], F32R)
        ctl = sb("ctl", [P, KD, NE], F32)
        bo_row = sb("bo_row", [P, D], F32)
        bias = sb("bias_sb", [P, E4], F32)
        ident = sb("ident3", [P, P], F32)
        tie = sb("tie", [P, GT], F32)
        blocks = sb("blocks3", [P, GQ], F32)
        o_raw = sb("o_raw", [P, 2, KD, P], F32)
        o_hi = sb("o_hi", [P, 2, KD, P], F32R)
        o_lo = sb("o_lo", [P, 2, KD, P], F32R)
        xb = sb("xb", [P, 2, D], F32)
        x2 = sb("x2", [P, 2, D], F32)
        xn = sb("xn3", [P, D], F32)
        xn_hi = sb("xn_hi", [P, 2, D], F32R)
        xn_lo = sb("xn_lo", [P, 2, D], F32R)
        xn_t = sb("xn_t", [P, 2, KD, P], F32)
        stats = sb("stats3", [P, 6], F32)
        mv = sb("mv3", [P, 2], F32)
        ve = sb("ve3", [P, 1], F32)
        sd = sb("sd3", [P, 1], F32)
        r0 = sb("r03", [P, 1], F32)
        r1 = sb("r13", [P, 1], F32)
        rstd = sb("rstd3", [P, 1], F32)
        gate = sb("gate3", [P, 1], F32)
        logits = sb("logits", [P, P], F32)
        best = sb("best", [P, GQ], F32)
        pick_t = sb("pick_t", [P, 2, P], F32)
        pick = sb("pick", [P, 2, GQ, NE], F32R)
        bank = ctx.enter_context(nc.psum_tensor("p3_bank", [P, 8, 512], F32))
        A, TB, LB, DB, EB, FB = 0, 2, 3, 4, 5, (7, 4)

        const_in = sem("c3_in")
        f1_in = sem("f1_in")
        wo_split = sem("wo_split")
        o_loaded = [sem(f"o_loaded{i}") for i in range(2)]
        x_loaded = [sem(f"x3_loaded{i}") for i in range(2)]
        x2_stored = [sem(f"x2_stored{i}") for i in range(2)]
        pick_stored = [sem(f"pick_stored{i}") for i in range(2)]
        o_hi_done = sem("o_hi_done")
        o_lo_done = sem("o_lo_done")
        xb_done = sem("xb_done")
        attended = sem("attended")
        x2_done = sem("x2_done")
        chain = sem("chain3")
        sd_done = sem("sd3_done")
        xn_done = sem("xn3_done")
        xn_hi_done = sem("xn3_hi_done")
        xn_lo_done = sem("xn3_lo_done")
        turned = sem("turned")
        xn_t_done = sem("xn_t_done")
        routed = sem("routed")
        tie_done = sem("tie_done")
        best_done = sem("best_done")
        pick_t_done = sem("pick_t_done")
        pick_turned = sem("pick_turned")
        pick_done = sem("pick_done")
        gathered = sem("gathered")
        taken_a = sem("taken_a")
        taken_v = sem("taken_v")
        hidden = sem("hidden")
        biased = sem("biased")
        relued = sem("relued")

        o_src = m.o.rearrange("g p (i s) -> i p g s", s=P)
        x_src = a.x.rearrange("b s d -> (b s) d").rearrange("(i p) d -> i p d", p=P)
        x2_dst = m.x2.rearrange("(i p) d -> i p d", p=P)

        with nc.Block() as block:
            @block.sync
            def _(sp):
                for dst, src in ((wo_raw, a.wo_t.rearrange("(k p) n -> p k n", p=P)),
                                 (ident[:], a.ident), (ctl[:], a.controller.rearrange("(k p) n -> p k n", p=P)),
                                 (bo_row[:], a.bo.unsqueeze(0).broadcast_to([P, D])),
                                 (tie[:], a.tie_row.unsqueeze(0).broadcast_to([P, GT])),
                                 (blocks[:], a.block_cols), (bias[:], a.bias_col)):
                    sp.dma_start(dst, src).then_inc(const_in, 16)

                def load(i, n, first):
                    tile, free = held(sp, i), held(sp, i - 1)
                    if not (first and n < 2):
                        sp.wait_ge(o_lo_done, free)
                    sp.dma_start(o_raw[:, n % 2], o_src[tile]).then_inc(o_loaded[n % 2], 16)
                    if not (first and n < 2):
                        sp.wait_ge(x2_done, free)
                    sp.dma_start(xb[:, n % 2], x_src[tile]).then_inc(x_loaded[n % 2], 16)

                load(0, 0, True)
                load(1, 1, True)
                sp.dma_start(f1[:], a.f1.rearrange("(k p) n -> p k n", p=P)).then_inc(f1_in, 16)
                for n in range(2, NT):
                    load(n, n, True)
                with sp.Fori(1, B) as b:
                    for n in range(NT):
                        load(b * NT + n, n, False)

            def stages(b, n):
                known = isinstance(b, int)
                return (not (known and b == B), not (known and b == 0 and n < 1) and not (known and b == B and n > 0),
                        not (known and b == 0 and n < 2))

            @block.gpsimd
            def _(pool):
                pool.wait_ge(const_in, 16 * 7)

                def o_part(b, n):
                    pool.wait_ge(o_hi_done, b * NT + n + 1)
                    pool.tensor_tensor(o_lo[:, n % 2], o_raw[:, n % 2], o_hi[:, n % 2].bitcast(F32),
                                       ALU.subtract).then_inc(o_lo_done, 1)

                def x_part(b, n):
                    pool.wait_ge(x_loaded[n % 2], (b * (NT // 2) + n // 2) * 16 + 16)
                    pool.tensor_tensor(xb[:, n % 2], xb[:, n % 2], bo_row[:], ALU.add).then_inc(xb_done, 1)

                def body(b, first, last):
                    for n in range(NT):
                        i = b * NT + n
                        if n < NT - 1 or not last:
                            o_part(b + (n + 1) // NT, (n + 1) % NT)
                            x_part(b + (n + 1) // NT, (n + 1) % NT)
                        pool.wait_ge(xn_hi_done, i + 1)
                        if not (first and n < 2):
                            pool.wait_ge(gathered, (i - 1) * KD)
                        pool.tensor_tensor(xn_lo[:, n % 2], xn[:], xn_hi[:, n % 2].bitcast(F32),
                                           ALU.subtract).then_inc(xn_lo_done, 1)

                o_part(0, 0)
                x_part(0, 0)
                body(0, True, False)
                with pool.Fori(1, B - 1) as b:
                    body(b, False, False)
                body(B - 1, False, True)

            @block.scalar
            def _(act):
                act.wait_ge(const_in, 16 * 7)
                act.copy(wo_hi[:], wo_raw).then_inc(wo_split, 1)

                def o_part(b, n, first):
                    act.wait_ge(o_loaded[n % 2], (b * (NT // 2) + n // 2) * 16 + 16)
                    if not (first and n < 2):
                        act.wait_ge(attended, b * NT + n - 1)
                    act.copy(o_hi[:, n % 2], o_raw[:, n % 2]).then_inc(o_hi_done, 1)

                def take(b, n, k):
                    act.wait_ge(gathered, (b * NT + n - 2) * KD + k + 1)
                    if n == 2 and k == 0 and not (isinstance(b, int) and b == 0):
                        act.wait_ge(hidden, b * 2)
                    to = (n - 2) % NT
                    act.copy(disp[:, k, :, to * GQ:(to + 1) * GQ].rearrange("p e g -> p g e"),
                             bank[:, EB + k % 2].rearrange("p (g e) -> p g e", g=GQ)).then_inc(taken_a, 1)

                def slot(b, n, first, last):
                    i = b * NT + n
                    head, middle, tail = stages(b, n)
                    if head and not (last and n == NT - 1):
                        o_part(b + (n + 1) // NT, (n + 1) % NT, first and n < 1)
                    if middle:
                        act.wait_ge(turned, i)
                        if not (first and n < 3):
                            act.wait_ge(routed, i - 2)
                        act.copy(xn_t[:, (n - 1) % 2], bank[:, TB]).then_inc(xn_t_done, 1)
                    if tail:
                        take(b, n, 0)
                    if head:
                        act.wait_ge(chain, i * CHAIN + 3)
                        act.activation(sd[:], ve[:], ACT.Sqrt).then_inc(sd_done, 1)
                    if tail:
                        take(b, n, 2)
                        take(b, n, 3)
                        act.dma_start(m.pick[i - 2], pick_t[:, n % 2]).then_inc(pick_stored[n % 2], 16)
                    if head:
                        act.dma_start(x2_dst[i], x2[:, n % 2]).then_inc(x2_stored[n % 2], 16)
                        act.wait_ge(xn_done, i + 1)
                        if not (first and n < 2):
                            act.wait_ge(gathered, (i - 1) * KD)
                        act.copy(xn_hi[:, n % 2], xn[:]).then_inc(xn_hi_done, 1)

                o_part(0, 0, True)
                for n in range(NT):
                    slot(0, n, True, False)
                with act.Fori(1, B - 1) as b:
                    for n in range(NT):
                        slot(b, n, False, False)
                for n in range(NT):
                    slot(B - 1, n, False, True)
                for n in range(2):
                    slot(B, n, False, True)
                for u in range(2):
                    act.wait_ge(x2_stored[u], 16 * B * NT // 2)
                    act.wait_ge(pick_stored[u], 16 * B * NT // 2)

            @block.vector
            def _(dve):
                dve.wait_ge(const_in, 16 * 7)
                dve.wait_ge(wo_split, 1)
                dve.tensor_tensor(wo_lo[:], wo_raw, wo_hi[:].bitcast(F32), ALU.subtract).then_inc(wo_split, 1)

                def link(i, n, ins):
                    ins.then_inc(chain, 1)
                    dve.wait_ge(chain, i * CHAIN + n)

                grouped = "p (g t) -> p g t"

                def choose(b, i, n, first):
                    dve.wait_ge(routed, i - 1)
                    if not (first and n == 2):
                        dve.wait_ge(pick_t_done, i - 2)
                    dve.tensor_tensor(logits[:].rearrange(grouped, g=GQ),
                                      bank[:, LB, 0:P].rearrange(grouped, g=GQ),
                                      tie[:].unsqueeze(1).broadcast_to([P, GQ, GT]),
                                      ALU.add).then_inc(tie_done, 1)
                    dve.wait_ge(tie_done, i - 1)
                    dve.tensor_reduce(best[:], logits[:].rearrange(grouped, g=GQ), AX.X,
                                      ALU.max).then_inc(best_done, 1)
                    if not (first and n < 4):
                        dve.wait_ge(pick_stored[n % 2], (b * (NT // 2) + (n - 2) // 2) * 16)
                        dve.wait_ge(pick_turned, i - 3)
                    dve.wait_ge(best_done, i - 1)
                    dve.tensor_tensor(pick_t[:, n % 2].rearrange(grouped, g=GQ),
                                      logits[:].rearrange(grouped, g=GQ),
                                      best[:].unsqueeze(2).broadcast_to([P, GQ, GT]),
                                      ALU.is_equal).then_inc(pick_t_done, 1)
                    dve.wait_ge(pick_turned, i - 1)
                    if not (first and n < 4):
                        dve.wait_ge(gathered, (i - 3) * KD)
                    dve.tensor_tensor(pick[:, n % 2],
                                      bank[:, DB, 0:NE].unsqueeze(1).broadcast_to([P, GQ, NE]),
                                      blocks[:].unsqueeze(2).broadcast_to([P, GQ, NE]),
                                      ALU.mult).then_inc(pick_done, 1)

                def slot(b, n, first):
                    i = b * NT + n
                    head, _, tail = stages(b, n)
                    if tail:
                        choose(b, i, n, first)
                    if head:
                        dve.wait_ge(attended, i + 1)
                        dve.wait_ge(xb_done, i + 1)
                        if not (first and n < 2):
                            dve.wait_ge(x2_stored[n % 2], (b * (NT // 2) + n // 2) * 16)
                        dve.tensor_tensor(x2[:, n % 2], bank[:, A + n % 2], xb[:, n % 2],
                                          ALU.add).then_inc(x2_done, 1)
                        dve.wait_ge(x2_done, i + 1)
                        link(i, 1, dve.bn_stats(stats[:], x2[:, n % 2]))
                        dve.memset(gate[:], 0.0)
                        link(i, 2, dve.bn_aggr(mv[:], stats[:]))
                        dve.tensor_scalar(ve[:], mv[:, 1:2], EPS, None, ALU.add).then_inc(chain, 1)
                    if tail:
                        dve.wait_ge(gathered, (i - 2) * KD + 2)
                        to = (n - 2) % NT
                        dve.tensor_copy(disp[:, 1, :, to * GQ:(to + 1) * GQ].rearrange("p e g -> p g e"),
                                        bank[:, EB + 1].rearrange("p (g e) -> p g e", g=GQ)).then_inc(taken_v, 1)
                    if head:
                        dve.wait_ge(sd_done, i + 1)
                        link(i, 4, dve.reciprocal(r0[:], sd[:]))
                        link(i, 5, dve.scalar_tensor_tensor(r1[:], r0[:], r0[:, 0:1], ve[:], ALU.mult, ALU.mult))
                        link(i, 6, dve.tensor_scalar(r1[:], r1[:], -0.5, 1.5, ALU.mult, ALU.add))
                        link(i, 7, dve.tensor_tensor(rstd[:], r0[:], r1[:], ALU.mult))
                        if not (first and n < 1):
                            dve.wait_ge(xn_lo_done, i)
                            dve.wait_ge(turned, i)
                        dve.tensor_scalar(xn[:], x2[:, n % 2], mv[:, 0:1], rstd[:], ALU.subtract,
                                          ALU.mult).then_inc(xn_done, 1)
                    if n == 1 and not first:
                        layer_one(b)

                def layer_one(b):
                    for half in range(2):
                        es = slice(half * (E4 // 2), (half + 1) * (E4 // 2))
                        dve.wait_ge(hidden, b * 2 + half - 1)
                        to = inner[:, es, :].rearrange("p e (b g) -> p b e g", b=B)[:, b - 1]
                        dve.tensor_tensor(to, bank[:, FB[half]].rearrange("p (e g) -> p e g", g=GB),
                                          bias[:, es].unsqueeze(2).broadcast_to([P, E4 // 2, GB]),
                                          ALU.add).then_inc(biased, 1)
                        dve.wait_ge(biased, b * 2 + half - 1)
                        dve.tensor_scalar(to, to, 0.0, None, ALU.max).then_inc(relued, 1)

                for n in range(NT):
                    slot(0, n, True)
                with dve.Fori(1, B) as b:
                    for n in range(NT):
                        slot(b, n, False)
                for n in range(2):
                    slot(B, n, False)

            @block.tensor
            def _(pe):
                pe.wait_ge(wo_split, 2)

                def project_out(n, ks):
                    for k in ks:
                        oh, ol = o_hi[:, n % 2, k], o_lo[:, n % 2, k]
                        pe.matmul(bank[:, A + n % 2], oh, wo_hi[:, k], start=(k == 0), stop=False)
                        pe.matmul(bank[:, A + n % 2], oh, wo_lo[:, k], start=False, stop=False)
                        mm = pe.matmul(bank[:, A + n % 2], ol, wo_hi[:, k], start=False, stop=(k == KD - 1))
                    return mm

                def gather(i, n, first, ks):
                    for k in ks:
                        oldest = first and n == 2
                        if k == 0 and not oldest:
                            pe.wait_ge(taken_a, (i - 2) * 3 - 1)
                        if k == 1 and not oldest:
                            pe.wait_ge(taken_a, (i - 2) * 3)
                        if k == 2:
                            pe.wait_ge(taken_a, (i - 2) * 3 + 1)
                        if k == 3:
                            pe.wait_ge(taken_v, i - 1)
                        out = bank[:, EB + k % 2]
                        rhs = pick[:, n % 2].rearrange("p g e -> p (g e)")
                        pe.matmul(out, xn_hi[:, n % 2, k * P:(k + 1) * P], rhs, start=True, stop=False)
                        pe.matmul(out, xn_lo[:, n % 2, k * P:(k + 1) * P], rhs, start=False,
                                  stop=True).then_inc(gathered, 1)

                def slot(b, n, first):
                    i = b * NT + n
                    head, middle, tail = stages(b, n)
                    if head:
                        pe.wait_ge(o_lo_done, i + 1)
                        if not (first and n < 2):
                            pe.wait_ge(x2_done, i - 1)
                        project_out(n, range(0, KD // 2))
                    if tail:
                        pe.wait_ge(pick_t_done, i - 1)
                        if n == 2 and not first:
                            pe.wait_ge(biased, b * 2)
                        if not (first and n == 2):
                            pe.wait_ge(pick_done, i - 2)
                        pe.transpose(bank[:, DB, 0:P], pick_t[:, n % 2], ident[:]).then_inc(pick_turned, 1)
                    if head:
                        project_out(n, range(KD // 2, KD)).then_inc(attended, 1)
                    if middle:
                        pe.wait_ge(xn_done, i)
                        if not (first and n == 1):
                            pe.wait_ge(xn_t_done, i - 1)
                        for k in range(KD):
                            mm = pe.transpose(bank[:, TB, k * P:(k + 1) * P], xn[:, k * P:(k + 1) * P], ident[:])
                        mm.then_inc(turned, 1)
                    if tail:
                        pe.wait_ge(xn_lo_done, i - 1)
                        pe.wait_ge(pick_done, i - 1)
                        gather(i, n, first, (0, 1))
                    if middle:
                        pe.wait_ge(xn_t_done, i)
                        if not (first and n == 1):
                            pe.wait_ge(tie_done, i - 1)
                        for k in range(KD):
                            mm = pe.matmul(bank[:, LB, 0:P], ctl[:, k], xn_t[:, (n - 1) % 2, k],
                                           start=(k == 0), stop=(k == KD - 1))
                        mm.then_inc(routed, 1)
                    if tail:
                        gather(i, n, first, (2, 3))
                    if n == 1 and not first:
                        layer_one(b)

                def layer_one(b):
                    pe.wait_ge(f1_in, 16)
                    pe.wait_ge(taken_a, b * NT * 3)
                    pe.wait_ge(taken_v, b * NT)
                    for half in range(2):
                        for e in range(E4 // 2):
                            for k in range(KD):
                                for q in range(4):
                                    es = q * E4 + half * (E4 // 2) + e
                                    mm = pe.matmul(bank[q * F:(q + 1) * F, FB[half], e * GB:(e + 1) * GB],
                                                   f1[:, k, es * F:(es + 1) * F], disp[:, k, es],
                                                   start=(k == 0), stop=(k == KD - 1), tile_position=(0, q * F),
                                                   skip_group_check=True)
                        mm.then_inc(hidden, 1)

                for n in range(NT):
                    slot(0, n, True)
                with pe.Fori(1, B) as b:
                    for n in range(NT):
                        slot(b, n, False)
                for n in range(2):
                    slot(B, n, False)


def expand(nc, a, m, inner):
    GB = S // GT
    NT = S // P
    GQ = P // GT
    RING = 4
    STAGE = 8
    AHEAD = 3
    COMBINE = 5
    NDMA = 16

    with ExitStack() as ctx:
        def sb(name, shape, dt):
            return ctx.enter_context(nc.sbuf_tensor(name, shape, dt))

        def sem(name):
            return ctx.enter_context(nc.semaphore(name))

        f2 = sb("f2_sb", [P, E4, D], F32)
        y = sb("y_rows", [P, GB, D], F32)
        in_hi = sb("in_hi", [P, E4, GB], F32R)
        blocks = sb("blocks4", [P, 4], F32)
        w_hi = sb("f2_hi", [P, RING, D], F32R)
        w_lo = sb("f2_lo", [P, RING, D], F32R)
        d_hi = sb("d_hi", [P, 2, 2, 4, GB], F32R)
        d_lo = sb("d_lo", [P, 2, 2, 4, GB], F32R)
        stage = sb("y_stage", [P, STAGE, D], F32)
        pick = sb("pick_in", [P, NT, P], F32)
        x2 = sb("x2_in", [P, NT, D], F32)
        bank = ctx.enter_context(nc.psum_tensor("p4_bank", [P, 8, 512], F32))

        c_in = sem("c4_in")
        f2_in = [sem(f"f2_in{i}") for i in range(NDMA)]
        pick_in = sem("pick_in_sem")
        x_in = sem("x4_in")
        in_hi_done = sem("in_hi_done")
        in_lo_done = sem("in_lo_done")
        w_hi_done = sem("f2_hi_done")
        w_lo_v = sem("f2_lo_v")
        w_lo_p = sem("f2_lo_p")
        d_hi_done = sem("d_hi_done")
        d_lo_done = sem("d_lo_done")
        made = sem("y_made")
        staged_a = sem("y_staged_a")
        staged_v = sem("y_staged_v")
        moved = [sem(f"y_moved{i}") for i in range(STAGE)]
        summed = sem("summed")
        added = sem("added")
        stored = sem("out_stored")

        x2_src = m.x2.rearrange("(b n p) d -> b p n d", b=B, p=P)
        o_dst = a.out.rearrange("b (n p) d -> b p n d", p=P)
        values = inner[:].rearrange("p e (b g) -> p b e g", b=B)
        p_src = m.pick.rearrange("(b n) e t -> b e n t", b=B)
        JL = E4 // NDMA

        with nc.Block() as block:
            @block.sync
            def _(sp):
                sp.dma_start(blocks[:], a.block_cols).then_inc(c_in, 16)

                def load(i):
                    sp.dma_start(f2[:, i * JL:(i + 1) * JL], a.f2[:, i * JL:(i + 1) * JL]).then_inc(f2_in[i], 16)

                for i in range(4):
                    load(i)

                def results(b):
                    for n in range(0, NT, 2):
                        cur, done = held(sp, b - 1), held(sp, (b - 1) * NT + n + 2)
                        sp.wait_ge(added, done)
                        sp.dma_start(o_dst[cur][:, n:n + 2], x2[:, n:n + 2]).then_inc(stored, 16)

                def move(b, first):
                    base, cur = held(sp, b * (E4 // 2)), held(sp, b)
                    all_stored = held(sp, b * (NT // 2) * 16)
                    for j in range(E4):
                        sp.wait_ge((staged_a, staged_v)[j % 2], base + j // 2 + 1)
                        sp.dma_start(y[j::E4], stage[:, j % STAGE]).then_inc(moved[j % STAGE], 16)
                        if first and j % JL == 1 and j // JL + 4 < NDMA:
                            load(j // JL + 4)
                        if j == E4 // 2 - 2:
                            sp.dma_start(pick[:], p_src[cur]).then_inc(pick_in, 16)
                            if not first:
                                sp.wait_ge(stored, all_stored)
                        if j >= E4 // 2 and j % 2 == 0:
                            n = (j - E4 // 2) // 2
                            sp.dma_start(x2[:, n], x2_src[cur][:, n]).then_inc(x_in, 16)

                move(0, True)
                with sp.Fori(1, B) as b:
                    results(b)
                    move(b, False)
                results(B)
                sp.wait_ge(stored, B * (NT // 2) * 16)

            @block.gpsimd
            def _(pool):
                pool.wait_ge(c_in, 16)

                def prepare(b, j, first):
                    if j % 2 == 0:
                        if j == 0:
                            pool.wait_ge(in_lo_done, b + 1)
                        if not (first and j < 4):
                            pool.wait_ge(made, b * E4 + j - 2)
                        src = values[:, b, j:j + 2].unsqueeze(2).broadcast_to([P, 2, 4, GB])
                        pool.tensor_tensor(d_lo[:, j // 2 % 2], src,
                                           blocks[:].unsqueeze(1).unsqueeze(3).broadcast_to([P, 2, 4, GB]),
                                           ALU.mult).then_inc(d_lo_done, 1)
                    else:
                        pool.wait_ge(w_hi_done, b * E4 + j + 1)
                        pool.tensor_tensor(w_lo[:, j % RING], f2[:, j], w_hi[:, j % RING].bitcast(F32),
                                           ALU.subtract).then_inc(w_lo_p, 1)

                for j in range(E4):
                    prepare(0, j, True)
                with pool.Fori(1, B) as b:
                    for j in range(E4):
                        prepare(b, j, False)

            @block.scalar
            def _(act):
                def prepare(b, j, first):
                    if j == 0:
                        if not first:
                            act.wait_ge(d_hi_done, b * (E4 // 2))
                            act.wait_ge(in_lo_done, b)
                        act.copy(in_hi[:], values[:, b]).then_inc(in_hi_done, 1)
                    if first and j % JL == 0:
                        act.wait_ge(f2_in[j // JL], 16)
                    if not (first and j < RING):
                        act.wait_ge(made, b * E4 + j - RING + 1)
                        if j % 2 == 0:
                            act.wait_ge(w_lo_v, b * (E4 // 2) + j // 2 - 1)
                        else:
                            act.wait_ge(w_lo_p, b * (E4 // 2) + j // 2 - 1)
                    act.copy(w_hi[:, j % RING], f2[:, j]).then_inc(w_hi_done, 1)

                def body(b, first, last):
                    for j in range(E4):
                        nj = j + AHEAD
                        if nj < E4:
                            prepare(b, nj, first)
                        elif not last:
                            prepare(b + 1, nj - E4, False)
                        if j % 2 == 0:
                            act.wait_ge(made, b * E4 + j + 1)
                            if not (first and j < STAGE):
                                act.wait_ge(moved[j % STAGE], (b * (E4 // STAGE) + j // STAGE) * 16)
                            act.copy(stage[:, j % STAGE], bank[:, j % RING]).then_inc(staged_a, 1)

                for j in range(AHEAD):
                    prepare(0, j, True)
                body(0, True, False)
                with act.Fori(1, B - 1) as b:
                    body(b, False, False)
                body(B - 1, False, True)

            @block.vector
            def _(dve):
                dve.wait_ge(c_in, 16)

                def prepare(b, j, first):
                    if j % 2 == 0:
                        if j == 0:
                            dve.wait_ge(in_hi_done, b + 1)
                            dve.tensor_tensor(values[:, b], values[:, b], in_hi[:].bitcast(F32),
                                              ALU.subtract).then_inc(in_lo_done, 1)
                        if not (first and j < 4):
                            dve.wait_ge(made, b * E4 + j - 2)
                        src = in_hi[:, j:j + 2].bitcast(F32).unsqueeze(2).broadcast_to([P, 2, 4, GB])
                        dve.tensor_tensor(d_hi[:, j // 2 % 2], src,
                                          blocks[:].unsqueeze(1).unsqueeze(3).broadcast_to([P, 2, 4, GB]),
                                          ALU.mult).then_inc(d_hi_done, 1)
                        dve.wait_ge(w_hi_done, b * E4 + j + 1)
                        dve.tensor_tensor(w_lo[:, j % RING], f2[:, j], w_hi[:, j % RING].bitcast(F32),
                                          ALU.subtract).then_inc(w_lo_v, 1)

                def add(b):
                    dve.wait_ge(x_in, b * NT * 16)
                    for n in range(NT):
                        dve.wait_ge(summed, (b - 1) * NT + n + 1)
                        dve.tensor_tensor(x2[:, n], bank[:, RING + n % RING], x2[:, n], ALU.add).then_inc(added, 1)

                def body(b, first, last):
                    for j in range(E4):
                        nj = j + AHEAD
                        if nj < E4:
                            prepare(b, nj, first)
                        elif not last:
                            prepare(b + 1, nj - E4, False)
                        if j % 2 == 1:
                            dve.wait_ge(made, b * E4 + j + 1)
                            if not (first and j < STAGE):
                                dve.wait_ge(moved[j % STAGE], (b * (E4 // STAGE) + j // STAGE) * 16)
                            dve.tensor_copy(stage[:, j % STAGE], bank[:, j % RING]).then_inc(staged_v, 1)
                        if j == COMBINE and not first:
                            add(b)

                for j in range(AHEAD):
                    prepare(0, j, True)
                body(0, True, False)
                with dve.Fori(1, B - 1) as b:
                    body(b, False, False)
                body(B - 1, False, True)
                add(B)

            @block.tensor
            def _(pe):
                def make(b, j, first):
                    if j % 2 == 0:
                        pe.wait_ge(d_hi_done, b * (E4 // 2) + j // 2 + 1)
                        pe.wait_ge(d_lo_done, b * (E4 // 2) + j // 2 + 1)
                        pe.wait_ge(w_lo_v, b * (E4 // 2) + j // 2 + 1)
                    else:
                        pe.wait_ge(w_lo_p, b * (E4 // 2) + j // 2 + 1)
                    if not (first and j < RING):
                        pe.wait_ge((staged_a, staged_v)[j % 2], b * (E4 // 2) + j // 2 - 1)
                    to, r = bank[:, j % RING], j % RING
                    dh, dl = (d[:, j // 2 % 2, j % 2].rearrange("p q g -> p (q g)") for d in (d_hi, d_lo))
                    pe.matmul(to, dh, w_hi[:, r], start=True, stop=False)
                    pe.matmul(to, dh, w_lo[:, r], start=False, stop=False)
                    pe.matmul(to, dl, w_hi[:, r], start=False, stop=True).then_inc(made, 1)

                def combine(b, oldest):
                    pe.wait_ge(pick_in, b * 16)
                    for u in range(STAGE):
                        pe.wait_ge(moved[u], b * (E4 // STAGE) * 16)
                    for n in range(NT):
                        if not (oldest and n < RING):
                            pe.wait_ge(added, (b - 1) * NT + n - RING + 1)
                        for g in range(GQ):
                            mm = pe.matmul(bank[g * GT:(g + 1) * GT, RING + n % RING],
                                           pick[:, n, g * GT:(g + 1) * GT], y[:, n * GQ + g],
                                           start=True, stop=True, tile_position=(0, g * GT))
                        mm.then_inc(summed, 1)

                def body(b, first):
                    for j in range(E4):
                        make(b, j, first)
                        if j == COMBINE and not first:
                            combine(b, isinstance(b, int) and b == 1)

                body(0, True)
                body(1, False)
                with pe.Fori(2, B) as b:
                    body(b, False)
                combine(B, False)




def build(nc, a, m, phases=(1, 2, 3, 4)):
    if 1 in phases:
        project(nc, a, m)
    if 2 in phases:
        attend(nc, a, m)
    with nc.sbuf_tensor("inner", [P, E4, NGR], F32) as inner:
        for n, phase in ((3, dispatch), (4, expand)):
            if n in phases:
                phase(nc, a, m, inner)


def layout(**inputs):
    import numpy as np

    def arr(x):
        return np.ascontiguousarray(np.asarray(x))

    i = inputs
    ctx = arr(i["ctx_1024"])
    r = np.arange(P)
    ban = np.where(r[:, None] >= r[None, :], np.float32(MASKED), np.float32(0))
    ban0 = ban.copy()
    ban0[0, 0] = 0.0
    out = {
        "x": arr(i["x"]),
        "ctx_t": arr(ctx.reshape(NCH, CH, D).transpose(0, 2, 1)),
        "wq_t": arr(arr(i["L0_xattn_Wq"]).T),
        "wk_t": arr(arr(i["L0_xattn_Wk"]).T),
        "wv_t": arr(arr(i["L0_xattn_Wv"]).T),
        "wo_t": arr(arr(i["L0_xattn_Wo"]).T),
        "bv": arr(i["L0_xattn_bv"]),
        "bo": arr(i["L0_xattn_bo"]),
        "controller": arr(i["L0_ffn_controller"]).reshape(D, NE),
        "f1": arr(i["L0_ffn_f1"]).reshape(D, NE * F),
        "bias_col": arr(arr(i["L0_ffn_bias"]).reshape(4, E4, F).transpose(0, 2, 1)).reshape(P, E4),
        "f2": arr(arr(i["L0_ffn_f2"]).reshape(4, E4, F, D).transpose(0, 2, 1, 3)).reshape(P, E4, D),
        "ident": np.eye(P, dtype=np.float32),
        "mask_st": arr(np.stack([ban.T, ban0.T])),
        "tie_row": np.linspace(0.0, 1e-6, GT, dtype=np.float32),
        "block_cols": arr((r[:, None] // 32 == np.arange(4)[None, :]).astype(np.float32)),
    }
    return out


def kernel(**inputs):
    import numpy as np
    import concourse.bacc as bacc
    from concourse.bass_utils import run_bass_kernel_spmd

    nc = bacc.Bacc("TRN2", target_bir_lowering=False, num_devices=1)
    arrays, a = {}, Plan()
    for name, x in layout(**inputs).items():
        arrays["in_" + name] = x
        a.__dict__[name] = nc.dram_tensor("in_" + name, x.shape, mybir.dt.from_np(x.dtype), kind="ExternalInput").ap()
    a.out = nc.dram_tensor("out", (B, S, D), F32, kind="ExternalOutput").ap()
    build(nc, a, scratch(nc))
    r = run_bass_kernel_spmd(nc, [arrays], core_ids=[0])
    return r.results[0]["out"]
```
